# Optimizing a Trainium2 kernel written in Bass

```python
import numpy as np
import jax
import jax.numpy as jnp

def _softmax(x, axis=-1):
    return jax.nn.softmax(x, axis=axis)

def _gelu(x):
    return jax.nn.gelu(x, approximate=True)

def _silu(x):
    return jax.nn.silu(x)

def _sigmoid(x):
    return jax.nn.sigmoid(x)

def _layernorm(x, axis=-1, eps=1e-05):
    m = jnp.mean(x, axis=axis, keepdims=True)
    v = jnp.var(x, axis=axis, keepdims=True)
    return (x - m) / jnp.sqrt(v + eps)

def _scatter_add(tgt, idx, src, axis=0):
    return tgt.at[idx].add(src)

def _segment_sum(src, seg, n):
    return jax.ops.segment_sum(src, seg, n)
kernel_name = 'mk_xattn_seq_d4_seqx_r8_3a2d96'

def setup_inputs(seed: int=0):
    np.random.seed(seed)
    _w = jnp.asarray

    def _rec_inputs():
        import jax
        import jax.numpy as jnp
        _rk = jax.random.key(seed)
        x = 7.22e-05 + 1 * jax.random.normal(jax.random.fold_in(_rk, 1), (8, 100, 128), jnp.float32)
        _lenS = 100 - jax.random.randint(jax.random.fold_in(_rk, 7), (8,), 0, max(1, 100 // 4) + 1, jnp.int32)
        _lenS2 = 1444 - jax.random.randint(jax.random.fold_in(_rk, 8), (8,), 0, max(1, 1444 // 4) + 1, jnp.int32)
        _ctx_1024P = jax.random.normal(jax.random.fold_in(_rk, 11), (8, 16, 128), jnp.float32)
        _ctx_1024c = jax.random.dirichlet(jax.random.fold_in(_rk, 511), 0.3 * jnp.ones((16,), jnp.float32), (8, 1444))
        _ctx_1024t = jnp.einsum('bsk,bkd->bsd', _ctx_1024c, _ctx_1024P)
        _ctx_1024t = _ctx_1024t * jax.lax.rsqrt(jnp.mean(jnp.square(_ctx_1024t)) + 1e-12) * 0.953939
        ctx_1024 = 4.13588e-05 + 0.999923 * (_ctx_1024t + 0.3 * jax.random.normal(jax.random.fold_in(_rk, 611), (8, 1444, 128), jnp.float32))
        _validS = jnp.arange(100)[None, :] < _lenS[:, None]
        _validS2 = jnp.arange(1444)[None, :] < _lenS2[:, None]
        _causal = jnp.tril(jnp.ones((100, 100), dtype=bool))
        mask_Bx1xSxS2_bf0 = jnp.logical_not(jnp.ones((8, 1, 100, 1444), dtype=bool))
        return (x, ctx_1024, mask_Bx1xSxS2_bf0)
    x, ctx_1024, mask_Bx1xSxS2_bf0 = _rec_inputs()

    def _L0_xattn_setup():
        import jax, jax.numpy as jnp
        import numpy as np
        D_MODEL = 128
        NUM_HEADS = 16
        HEAD_DIM = D_MODEL // NUM_HEADS
        EPS = 1e-06

        def rmsnorm(x, w):
            xf = x.astype(jnp.float32)
            n = xf * jax.lax.rsqrt(jnp.mean(xf * xf, axis=-1, keepdims=True) + EPS)
            return (n * w.astype(jnp.float32)).astype(x.dtype)
        key = jax.random.key(seed)
        ks = jax.random.split(key, 8)
        B, S, K = (4, 256, 256)
        s = 1.0 / np.sqrt(D_MODEL)
        return {'x': jax.random.normal(ks[0], (B, S, D_MODEL), jnp.float32), 'kv': jax.random.normal(ks[1], (B, K, D_MODEL), jnp.float32), 'wq': jax.random.normal(ks[2], (D_MODEL, D_MODEL), jnp.float32) * s, 'wk': jax.random.normal(ks[3], (D_MODEL, D_MODEL), jnp.float32) * s, 'wv': jax.random.normal(ks[4], (D_MODEL, D_MODEL), jnp.float32) * s, 'wo': jax.random.normal(ks[5], (D_MODEL, D_MODEL), jnp.float32) * s, 'bo': jnp.zeros((D_MODEL,), jnp.float32), 'gq': jnp.ones((D_MODEL,), jnp.float32), 'gkv': jnp.ones((D_MODEL,), jnp.float32)}
    _L0_xattn_all = _L0_xattn_setup()
    _L0_xattn_in = {k: v for k, v in _L0_xattn_all.items() if k in ('wq', 'wk', 'wv', 'wo', 'bo', 'gq', 'gkv')}
    del _L0_xattn_all

    def _L1_xattn_setup():
        import jax, jax.numpy as jnp
        import numpy as np
        N_HEAD = 16
        MODEL_DIM = 128
        HEAD_DIM = MODEL_DIM // N_HEAD
        B, S = (4, 256)
        LN_EPS = 1e-05

        def _split_heads(x):
            b, s, _ = x.shape
            return x.reshape(b, s, N_HEAD, HEAD_DIM).transpose(0, 2, 1, 3)
        key = jax.random.key(seed)
        ks = jax.random.split(key, 16)
        sc = 0.02
        return {'q': jax.random.normal(ks[0], (B, S, MODEL_DIM), jnp.float32), 'k': jax.random.normal(ks[1], (B, S, MODEL_DIM), jnp.float32), 'v': jax.random.normal(ks[2], (B, S, MODEL_DIM), jnp.float32), 'mask': jnp.zeros((B, 1, S, S), dtype=bool), 'training': 0, 'Wq': jax.random.normal(ks[3], (MODEL_DIM, MODEL_DIM), jnp.float32) * sc, 'bq': jnp.zeros((MODEL_DIM,), jnp.float32), 'Wk': jax.random.normal(ks[4], (MODEL_DIM, MODEL_DIM), jnp.float32) * sc, 'bk': jnp.zeros((MODEL_DIM,), jnp.float32), 'Wv': jax.random.normal(ks[5], (MODEL_DIM, MODEL_DIM), jnp.float32) * sc, 'bv': jnp.zeros((MODEL_DIM,), jnp.float32), 'Wo': jax.random.normal(ks[6], (MODEL_DIM, MODEL_DIM), jnp.float32) * sc, 'bo': jnp.zeros((MODEL_DIM,), jnp.float32), 'gamma': jnp.ones((MODEL_DIM,), jnp.float32), 'beta': jnp.zeros((MODEL_DIM,), jnp.float32)}
    _L1_xattn_all = _L1_xattn_setup()
    _L1_xattn_in = {k: v for k, v in _L1_xattn_all.items() if k in ('Wq', 'bq', 'Wk', 'bk', 'Wv', 'bv', 'Wo', 'bo', 'gamma', 'beta')}
    del _L1_xattn_all

    def _L2_xattn_setup():
        import jax, jax.numpy as jnp
        import numpy as np
        B, S, D_MODEL, H, D_FF = (2, 256, 128, 16, 512)
        D_HEAD = D_MODEL // H
        LN_EPS = 1e-05

        def _xavier(key, shape):
            fan_out, fan_in = shape
            std = (2.0 / (fan_in + fan_out)) ** 0.5
            return jax.random.normal(key, shape, dtype=jnp.float32) * std

        def _layer_norm(x, g, b):
            mu = jnp.mean(x, axis=-1, keepdims=True)
            var = jnp.mean((x - mu) ** 2, axis=-1, keepdims=True)
            return (x - mu) * jax.lax.rsqrt(var + LN_EPS) * g + b
        key = jax.random.key(seed)
        ks = jax.random.split(key, 8)
        return {'q': jax.random.normal(ks[0], (B, S, D_MODEL), dtype=jnp.float32), 'k': jax.random.normal(ks[1], (B, S, D_MODEL), dtype=jnp.float32), 'Wq': _xavier(ks[2], (D_MODEL, D_MODEL)), 'bq': jnp.zeros((D_MODEL,), jnp.float32), 'Wk': _xavier(ks[3], (D_MODEL, D_MODEL)), 'bk': jnp.zeros((D_MODEL,), jnp.float32), 'Wv': _xavier(ks[4], (D_MODEL, D_MODEL)), 'bv': jnp.zeros((D_MODEL,), jnp.float32), 'W1': _xavier(ks[5], (D_FF, D_MODEL)), 'b1': jnp.zeros((D_FF,), jnp.float32), 'W2': _xavier(ks[6], (D_MODEL, D_FF)), 'b2': jnp.zeros((D_MODEL,), jnp.float32), 'ln_g': jnp.ones((D_MODEL,), jnp.float32), 'ln_b': jnp.zeros((D_MODEL,), jnp.float32), 'use_causal_mask': 1}
    _L2_xattn_all = _L2_xattn_setup()
    _L2_xattn_in = {k: v for k, v in _L2_xattn_all.items() if k in ('Wq', 'bq', 'Wk', 'bk', 'Wv', 'bv', 'W1', 'b1', 'W2', 'b2', 'ln_g', 'ln_b')}
    del _L2_xattn_all

    def _L3_xattn_setup():
        import jax, jax.numpy as jnp
        import numpy as np
        H = 16
        D = 128
        DK = D // H
        key = jax.random.key(seed)
        ks = jax.random.split(key, 10)
        B, S = (2, 256)
        scale = 1.0 / np.sqrt(D)
        inp = {'query': jax.random.normal(ks[0], (B, S, D), jnp.float32), 'key_': jax.random.normal(ks[1], (B, S, D), jnp.float32), 'value': jax.random.normal(ks[2], (B, S, D), jnp.float32), 'Wq': jax.random.normal(ks[3], (D, D), jnp.float32) * scale, 'bq': jnp.zeros((D,), jnp.float32), 'Wk': jax.random.normal(ks[4], (D, D), jnp.float32) * scale, 'bk': jnp.zeros((D,), jnp.float32), 'Wv': jax.random.normal(ks[5], (D, D), jnp.float32) * scale, 'bv': jnp.zeros((D,), jnp.float32), 'ln_gamma': jnp.ones((D,), jnp.float32), 'ln_beta': jnp.zeros((D,), jnp.float32)}
        return inp
    _L3_xattn_all = _L3_xattn_setup()
    _L3_xattn_in = {k: v for k, v in _L3_xattn_all.items() if k in ('Wq', 'bq', 'Wk', 'bk', 'Wv', 'bv', 'ln_gamma', 'ln_beta')}
    del _L3_xattn_all
    return {'x': x, 'ctx_1024': ctx_1024, 'mask_Bx1xSxS2_bf0': mask_Bx1xSxS2_bf0, 'L0_xattn_wq': _L0_xattn_in['wq'], 'L0_xattn_wk': _L0_xattn_in['wk'], 'L0_xattn_wv': _L0_xattn_in['wv'], 'L0_xattn_wo': _L0_xattn_in['wo'], 'L0_xattn_bo': _L0_xattn_in['bo'], 'L0_xattn_gq': _L0_xattn_in['gq'], 'L0_xattn_gkv': _L0_xattn_in['gkv'], 'L1_xattn_Wq': _L1_xattn_in['Wq'], 'L1_xattn_bq': _L1_xattn_in['bq'], 'L1_xattn_Wk': _L1_xattn_in['Wk'], 'L1_xattn_bk': _L1_xattn_in['bk'], 'L1_xattn_Wv': _L1_xattn_in['Wv'], 'L1_xattn_bv': _L1_xattn_in['bv'], 'L1_xattn_Wo': _L1_xattn_in['Wo'], 'L1_xattn_bo': _L1_xattn_in['bo'], 'L1_xattn_gamma': _L1_xattn_in['gamma'], 'L1_xattn_beta': _L1_xattn_in['beta'], 'L2_xattn_Wq': _L2_xattn_in['Wq'], 'L2_xattn_bq': _L2_xattn_in['bq'], 'L2_xattn_Wk': _L2_xattn_in['Wk'], 'L2_xattn_bk': _L2_xattn_in['bk'], 'L2_xattn_Wv': _L2_xattn_in['Wv'], 'L2_xattn_bv': _L2_xattn_in['bv'], 'L2_xattn_W1': _L2_xattn_in['W1'], 'L2_xattn_b1': _L2_xattn_in['b1'], 'L2_xattn_W2': _L2_xattn_in['W2'], 'L2_xattn_b2': _L2_xattn_in['b2'], 'L2_xattn_ln_g': _L2_xattn_in['ln_g'], 'L2_xattn_ln_b': _L2_xattn_in['ln_b'], 'L3_xattn_Wq': _L3_xattn_in['Wq'], 'L3_xattn_bq': _L3_xattn_in['bq'], 'L3_xattn_Wk': _L3_xattn_in['Wk'], 'L3_xattn_bk': _L3_xattn_in['bk'], 'L3_xattn_Wv': _L3_xattn_in['Wv'], 'L3_xattn_bv': _L3_xattn_in['bv'], 'L3_xattn_ln_gamma': _L3_xattn_in['ln_gamma'], 'L3_xattn_ln_beta': _L3_xattn_in['ln_beta']}

def reference(x, ctx_1024, mask_Bx1xSxS2_bf0, L0_xattn_wq, L0_xattn_wk, L0_xattn_wv, L0_xattn_wo, L0_xattn_bo, L0_xattn_gq, L0_xattn_gkv, L1_xattn_Wq, L1_xattn_bq, L1_xattn_Wk, L1_xattn_bk, L1_xattn_Wv, L1_xattn_bv, L1_xattn_Wo, L1_xattn_bo, L1_xattn_gamma, L1_xattn_beta, L2_xattn_Wq, L2_xattn_bq, L2_xattn_Wk, L2_xattn_bk, L2_xattn_Wv, L2_xattn_bv, L2_xattn_W1, L2_xattn_b1, L2_xattn_W2, L2_xattn_b2, L2_xattn_ln_g, L2_xattn_ln_b, L3_xattn_Wq, L3_xattn_bq, L3_xattn_Wk, L3_xattn_bk, L3_xattn_Wv, L3_xattn_bv, L3_xattn_ln_gamma, L3_xattn_ln_beta):
    import jax
    import jax.numpy as jnp

    def _L0_xattn_ref(x, kv, wq, wk, wv, wo, bo, gq, gkv):
        import jax, jax.numpy as jnp
        import numpy as np
        D_MODEL = 128
        NUM_HEADS = 16
        HEAD_DIM = D_MODEL // NUM_HEADS
        EPS = 1e-06

        def rmsnorm(x, w):
            xf = x.astype(jnp.float32)
            n = xf * jax.lax.rsqrt(jnp.mean(xf * xf, axis=-1, keepdims=True) + EPS)
            return (n * w.astype(jnp.float32)).astype(x.dtype)
        B, S, _ = x.shape
        K = kv.shape[1]
        xn = rmsnorm(x, gq)
        kvn = rmsnorm(kv, gkv)
        q = (xn @ wq.T).reshape(B, S, NUM_HEADS, HEAD_DIM)
        k = (kvn @ wk.T).reshape(B, K, NUM_HEADS, HEAD_DIM)
        v = (kvn @ wv.T).reshape(B, K, NUM_HEADS, HEAD_DIM)
        scale = HEAD_DIM ** (-0.5)
        scores = jnp.einsum('bshd,bkhd->bhsk', q, k) * scale
        attn = jax.nn.softmax(scores, axis=-1)
        o = jnp.einsum('bhsk,bkhd->bshd', attn, v).reshape(B, S, D_MODEL)
        out = o @ wo.T + bo
        return xn + out

    def _L1_xattn_ref(q, k, v, mask, training, Wq, bq, Wk, bk, Wv, bv, Wo, bo, gamma, beta):
        import jax, jax.numpy as jnp
        import numpy as np
        N_HEAD = 16
        MODEL_DIM = 128
        HEAD_DIM = MODEL_DIM // N_HEAD
        B, S = (4, 256)
        LN_EPS = 1e-05

        def _split_heads(x):
            b, s, _ = x.shape
            return x.reshape(b, s, N_HEAD, HEAD_DIM).transpose(0, 2, 1, 3)
        residual = q
        query = _split_heads(q @ Wq.T + bq)
        key = _split_heads(k @ Wk.T + bk)
        value = _split_heads(v @ Wv.T + bv)
        scale = 1.0 / (jnp.sqrt(jnp.float32(HEAD_DIM)) + 1e-08)
        score = jnp.einsum('bhqd,bhkd->bhqk', query, key) * scale
        score = jnp.where(mask, -jnp.inf, score)
        attn = jax.nn.softmax(score, axis=-1)
        ctx = jnp.einsum('bhqk,bhkd->bhqd', attn, value)
        ctx = ctx.transpose(0, 2, 1, 3).reshape(q.shape[0], q.shape[1], MODEL_DIM)
        o = ctx @ Wo.T + bo
        x = residual + o
        mu = jnp.mean(x, axis=-1, keepdims=True)
        var = jnp.mean(jnp.square(x - mu), axis=-1, keepdims=True)
        return (x - mu) / jnp.sqrt(var + LN_EPS) * gamma + beta

    def _L2_xattn_ref(q, k, Wq, bq, Wk, bk, Wv, bv, W1, b1, W2, b2, ln_g, ln_b, use_causal_mask):
        import jax, jax.numpy as jnp
        import numpy as np
        B, S, D_MODEL, H, D_FF = (2, 256, 128, 16, 512)
        D_HEAD = D_MODEL // H
        LN_EPS = 1e-05

        def _xavier(key, shape):
            fan_out, fan_in = shape
            std = (2.0 / (fan_in + fan_out)) ** 0.5
            return jax.random.normal(key, shape, dtype=jnp.float32) * std

        def _layer_norm(x, g, b):
            mu = jnp.mean(x, axis=-1, keepdims=True)
            var = jnp.mean((x - mu) ** 2, axis=-1, keepdims=True)
            return (x - mu) * jax.lax.rsqrt(var + LN_EPS) * g + b
        Bq, Sq, _ = q.shape
        Sk = k.shape[1]
        Q = q @ Wq.T + bq
        K = k @ Wk.T + bk
        V = k @ Wv.T + bv
        Q_ = Q.reshape(Bq, Sq, H, D_HEAD).transpose(0, 2, 1, 3)
        K_ = K.reshape(Bq, Sk, H, D_HEAD).transpose(0, 2, 1, 3)
        V_ = V.reshape(Bq, Sk, H, D_HEAD).transpose(0, 2, 1, 3)
        scores = jnp.einsum('bhqd,bhkd->bhqk', Q_, K_) / D_HEAD ** 0.5
        if use_causal_mask:
            causal = jnp.tril(jnp.ones((Sq, Sk), dtype=bool))
            scores = jnp.where(causal, scores, jnp.float32(-1000000000.0))
        sim = jax.nn.softmax(scores, axis=-1)
        att = jnp.einsum('bhqk,bhkd->bhqd', sim, V_)
        att_h = att.transpose(0, 2, 1, 3).reshape(Bq, Sq, D_MODEL)
        att_h = att_h + q
        att_h = _layer_norm(att_h, ln_g, ln_b)
        ff = jax.nn.gelu(att_h @ W1.T + b1, approximate=False) @ W2.T + b2
        return ff + att_h

    def _L3_xattn_ref(query, key_, value, Wq, bq, Wk, bk, Wv, bv, ln_gamma, ln_beta):
        import jax, jax.numpy as jnp
        import numpy as np
        H = 16
        D = 128
        DK = D // H
        B, S, _ = query.shape
        residual = query

        def proj(x, W, b):
            return (x @ W + b).reshape(B, -1, H, DK).transpose(0, 2, 1, 3)
        q = proj(query, Wq, bq)
        k = proj(key_, Wk, bk)
        v = proj(value, Wv, bv)
        scores = jnp.einsum('bhqd,bhkd->bhqk', q, k) / jnp.sqrt(jnp.float32(DK))
        p_att = jax.nn.softmax(scores, axis=-1)
        x = jnp.einsum('bhqk,bhkd->bhqd', p_att, v)
        x = x.transpose(0, 2, 1, 3).reshape(B, S, D)
        y = x + residual
        mu = jnp.mean(y, axis=-1, keepdims=True)
        var = jnp.var(y, axis=-1, keepdims=True)
        y = (y - mu) / jnp.sqrt(var + 1e-06)
        return y * ln_gamma + ln_beta
    x = _L0_xattn_ref(x, ctx_1024, L0_xattn_wq, L0_xattn_wk, L0_xattn_wv, L0_xattn_wo, L0_xattn_bo, L0_xattn_gq, L0_xattn_gkv)
    x = _L1_xattn_ref(x, ctx_1024, ctx_1024, mask_Bx1xSxS2_bf0, 0, L1_xattn_Wq, L1_xattn_bq, L1_xattn_Wk, L1_xattn_bk, L1_xattn_Wv, L1_xattn_bv, L1_xattn_Wo, L1_xattn_bo, L1_xattn_gamma, L1_xattn_beta)
    x = _L2_xattn_ref(x, ctx_1024, L2_xattn_Wq, L2_xattn_bq, L2_xattn_Wk, L2_xattn_bk, L2_xattn_Wv, L2_xattn_bv, L2_xattn_W1, L2_xattn_b1, L2_xattn_W2, L2_xattn_b2, L2_xattn_ln_g, L2_xattn_ln_b, 1)
    x = _L3_xattn_ref(x, ctx_1024, ctx_1024, L3_xattn_Wq, L3_xattn_bq, L3_xattn_Wk, L3_xattn_bk, L3_xattn_Wv, L3_xattn_bv, L3_xattn_ln_gamma, L3_xattn_ln_beta)
    return x

_drawn_inputs = setup_inputs


def setup_inputs(seed=0):
    import zlib

    import numpy as np

    out = dict(_drawn_inputs(seed))
    spreads = {'L0_xattn_bo': (0.0, 0.1),
     'L0_xattn_gq': (1.0, 0.2),
     'L0_xattn_gkv': (1.0, 0.2),
     'L1_xattn_bq': (0.0, 0.8),
     'L1_xattn_bk': (0.0, 0.8),
     'L1_xattn_bv': (0.0, 0.682),
     'L1_xattn_bo': (0.0, 0.1),
     'L1_xattn_gamma': (1.0, 0.2),
     'L1_xattn_beta': (0.0, 0.1),
     'L2_xattn_bq': (0.0, 0.381),
     'L2_xattn_bk': (0.0, 0.8),
     'L2_xattn_bv': (0.0, 0.1),
     'L2_xattn_b1': (0.0, 0.1),
     'L2_xattn_b2': (0.0, 0.1),
     'L2_xattn_ln_g': (1.0, 0.2),
     'L2_xattn_ln_b': (0.0, 0.1),
     'L3_xattn_bq': (0.0, 0.436),
     'L3_xattn_bk': (0.0, 0.8),
     'L3_xattn_bv': (0.0, 0.1),
     'L3_xattn_ln_gamma': (1.0, 0.2),
     'L3_xattn_ln_beta': (0.0, 0.1)}
    factors = {'L1_xattn_Wq': 8.0, 'L1_xattn_Wk': 8.0, 'L1_xattn_Wv': 3.193, 'L1_xattn_Wo': 2.713}
    for name, (base, spread) in spreads.items():
        noise = np.random.default_rng([zlib.crc32(name.encode()), seed]).standard_normal(out[name].shape)
        drawn = base * np.exp(spread * noise) if base else spread * noise
        out[name] = jnp.asarray(drawn.astype(out[name].dtype))
    for name, factor in factors.items():
        out[name] = (out[name] * factor).astype(out[name].dtype)
    return out
```

```python
from contextlib import ExitStack

import numpy as np

import concourse.bass as bass
from concourse import mybir

F32 = mybir.dt.float32
F16 = mybir.dt.float16
BF16 = mybir.dt.bfloat16
U8 = mybir.dt.uint8
I32 = mybir.dt.int32
ALU = mybir.AluOpType
ACT = mybir.ActivationFunctionType
AX = mybir.AxisListType.X

B, S, D = 8, 100, 128
KEYS = 1444
H, DH = 16, 8
T, HT = 4, 4
QW = HT * S
FF = 512
NCH = 12
LONG = KEYS - (KEYS // NCH) * NCH
ROWS = [KEYS // NCH + (c < LONG) for c in range(NCH)]
COL = [sum(ROWS[:c]) for c in range(NCH + 1)]
GROUPS = [range(0, 4), range(4, 8), range(8, 12)]
SCALE = float(DH) ** -0.5
MASKED = [-30000.0, -1e30]
VW = 32
PR, SR = 4, 2
PARTS = 3 * 32

ROW = {n: i for i, n in enumerate(
    ["gq", "bo0", "bv1", "bo1", "g1", "b1", "bv2", "g2", "b2", "ff2", "bv3", "g3", "b3"])}
COLC = {n: i for i, n in enumerate(["gkv", "bk1", "bk2", "bk3", "ffb0", "ffb1", "ffb2", "ffb3"])}

FULL = [("ct0", 0), ("ct1", 1), ("ct2", 2), ("k0", 0), ("k1", 1), ("k2", 2), ("v0", 0), ("v1", 1), ("v2", 2),
        ("xT", 0), ("q", 1), ("mt0", 0), ("mt1", 1), ("mn", 2), ("O", 0)]
MASK = [("mk0", 0), ("mk1", 1), ("mk2", 2)]
USES = [FULL + [("OT", 1), ("wo", 2)],
        FULL[:9] + MASK + FULL[9:] + [("OT", 1), ("wo", 2)],
        [("ct0", 0), ("k0", 1), ("v0", 2), ("xT", 0), ("q", 1), ("mt0", 0), ("mt1", 1), ("mn", 2), ("O", 0),
         ("OT", 1), ("h", 2), ("wo", 0)],
        FULL]
CHUNKS = [range(NCH), range(NCH), range(1), range(NCH)]
STEPS = [T * len(c) for c in CHUNKS]
OWN = [3, 7, 8, 8]
EPS = [1e-6, 1e-5, 1e-5, 1e-6]


def build(nc, ctx_in, x_in, mask_in, w_qkv, w_o, w_1, w_2, rows_in, cols_in, bq_in, headmask_in, ident_in, causal_in, out):
    with ExitStack() as es:
        def sb(name, shape, dt=F32):
            return es.enter_context(nc.sbuf_tensor(name, shape, dt))

        def psb(name):
            return es.enter_context(nc.psum_tensor(name, [128, 512], F32))

        def sem(name):
            return es.enter_context(nc.semaphore(name))

        wq = sb("wq", [128, 4, T, PARTS])
        wk = sb("wk", [128, 4, D])
        wv = sb("wv", [128, 4, D])
        wo = sb("wo", [128, 2, D])
        w1 = sb("w1", [128, FF])
        w2 = sb("w2", [128, FF // 128, D])
        W = {"k": wk, "v": wv}
        wq16 = sb("wq16", [128, 2, 4, T, PARTS], F16)
        wk16 = sb("wk16", [128, 2, 4, D], F16)
        wv16 = sb("wv16", [128, 2, 4, D], F16)
        rows = sb("rows", [S, len(ROW), D])
        cols = sb("cols", [128, len(COLC)])
        bq = sb("bq", [PARTS, 4, T])
        bqs = sb("bqs", [PARTS, 4, T])
        headmask = sb("headmask", [PARTS, HT])
        headmask16 = sb("headmask16", [PARTS, HT], F16)
        ident = sb("ident", [128, 128])
        ident16 = sb("ident16", [128, 128], F16)
        causal = sb("causal", [S, 2, S])
        half = sb("half", [128, NCH])
        identb = sb("identb", [128, 128], BF16)
        masked_by = sb("masked_by", [128, 2, 128], BF16)
        ones = sb("ones", [128, 1])
        anymask = sb("anymask", [128, B * S * KEYS // 128], U8)
        maskcount = sb("maskcount", [128, 1])
        maskflag = sb("maskflag", [1, 1], I32)
        mask8 = sb("mask8", [S, KEYS], U8)
        maskb = sb("maskb", [S, KEYS], BF16)
        maskT = sb("maskT", [128, NCH, S], BF16)
        xall = sb("xall", [S, B, D])
        nat = sb("nat", [128, NCH, D])
        sq = sb("sq", [128, NCH, D])
        ssq = sb("ssq", [128, NCH])
        rinv = sb("rinv", [128, NCH])
        ct = sb("ct", [128, 2, KEYS], F16)
        kp = sb("kp", [128, 2, KEYS], F16)
        krep = sb("krep", [PARTS + 1, T, KEYS], F16)
        vx = sb("vx", [128, NCH, H, VW])
        xcur = sb("xcur", [S, D])
        xT = sb("xT", [128, 2, S], F16)
        qf = sb("qf", [PARTS, T, S])
        qs = sb("qs", [PARTS, T, S], F16)
        qd = sb("qd", [PARTS, T, S], F16)
        qbd = sb("qbd", [PARTS + 1, T, HT, S], F16)
        mx = sb("mx", [128, T * QW], F16)
        mneg = sb("mneg", [S, H], F16)
        mrow = sb("mrow", [H, S], F16)
        masked = sb("masked", [S, 2, QW])
        probs = sb("probs", [128, PR, QW])
        osb = sb("osb", [128, QW])
        osum = sb("osum", [S, H])
        oatt = sb("oatt", [S, D])
        oT = sb("oT", [128, S])
        y = sb("y", [S, D])
        squared = sb("squared", [S, D])
        mv = sb("mv", [S, 2])
        vare = sb("vare", [S, 1])
        rstd = sb("rstd", [S, 1])
        xn = sb("xn", [S, D])
        hT = sb("hT", [128, FF // 128, S])
        outsb = sb("outsb", [S, D])

        bank = [psb(f"shared{i}") for i in range(3)]
        smax = [psb(f"smax{i}") for i in range(SR)]
        sexp = [psb(f"sexp{i}") for i in range(SR)]
        acc = psb("acc")

        const_in = sem("const_in")
        const_ready = sem("const_ready")
        x_power = sem("x_power")
        x_root = sem("x_root")
        vector_ready = sem("vector_ready")
        setup = sem("setup")
        OWNSEEN = [0] * 4
        ctx_loaded = sem("ctx_loaded")
        squares = sem("squares")
        row_power = sem("row_power")
        ctx_normal = sem("ctx_normal")
        filled = [sem(f"filled{i}") for i in range(3)]
        ct_hi = sem("ct_hi")
        ct_lo = sem("ct_lo")
        k_hi = sem("k_hi")
        k_lo = sem("k_lo")
        krep_in = sem("krep_in")
        x_copied = sem("x_copied")
        mask_in_all = sem("mask_in_all")
        mask_counted = sem("mask_counted")
        mask_summed = sem("mask_summed")
        flag_ready = sem("flag_ready")
        mask_loaded = sem("mask_loaded")
        mask_scaled = sem("mask_scaled")
        mask_ready = sem("mask_ready")
        x_hi = sem("x_hi")
        x_lo = sem("x_lo")
        q_read = sem("q_read")
        q_parts = sem("q_parts")
        q_spread = sem("q_spread")
        v_ready = sem("v_ready")
        smax_ready = sem("smax_ready")
        smax_used = sem("smax_used")
        m_ready = sem("m_ready")
        mrow_ready = sem("mrow_ready")
        mrow_in = sem("mrow_in")
        sexp_ready = sem("sexp_ready")
        masked_ready = sem("masked_ready")
        probs_ready = sem("probs_ready")
        pv_done = sem("pv_done")
        acc_copied = sem("acc_copied")
        o_read = sem("o_read")
        o_normal = sem("o_normal")
        wo_read = sem("wo_read")
        oT_ready = sem("oT_ready")
        var_ready = sem("var_ready")
        rstd_ready = sem("rstd_ready")
        h_ready = sem("h_ready")
        x_next = sem("x_next")
        out_ready = sem("out_ready")
        out_sent = sem("out_sent")
        dve_own = sem("dve_own")
        pool_own = sem("pool_own")

        G = [len(c) // 4 or 1 for c in CHUNKS]
        PER = {
            "ctx_loaded": [32, 32, 16, 32], "squares": [1, 0, 0, 0], "row_power": [1, 0, 0, 0],
            "ctx_normal": [1, 0, 0, 0], "ct_hi": G, "ct_lo": G, "k_hi": G, "k_lo": G,
            "krep_in": [16 * 12] * 4, "x_copied": [1] * 4, "x_hi": [1] * 4, "x_lo": [1] * 4, "q_parts": [1] * 4,
            "q_read": [1] * 4, "q_spread": [1] * 4, "v_ready": G, "smax_ready": STEPS, "smax_used": STEPS, "m_ready": [2] * 4,
            "mrow_ready": [1] * 4, "mrow_in": [16] * 4, "sexp_ready": STEPS, "masked_ready": [0, 0, 4, 0],
            "probs_ready": STEPS, "pv_done": STEPS, "acc_copied": [1] * 4, "o_read": [1] * 4, "o_normal": [0, 1, 1, 0],
            "wo_read": [1, 1, 1, 0],
            "oT_ready": [1, 1, 1, 0], "var_ready": [0, 1, 1, 1], "rstd_ready": [0, 1, 1, 1],
            "h_ready": [0, 0, 4, 0], "x_next": [1, 1, 1, 0], "out_ready": [0, 0, 0, 1], "out_sent": [0, 0, 0, 16],
            "mask_loaded": [0, 16, 0, 0], "mask_scaled": [0, 1, 0, 0], "mask_ready": [0, 3, 0, 0],
            "dve_own": OWN, "pool_own": [1, 0, 0, 0],
        }
        for i in range(3):
            PER[f"filled{i}"] = [sum(b == i for _, b in u) for u in USES]
        START = {"dve_own": 0, "pool_own": 2}
        READ = {"xT": (x_lo, "x_lo", 1), "q": (q_read, "q_read", 1), "mt0": (m_ready, "m_ready", 1),
                "mt1": (m_ready, "m_ready", 2), "mn": (mrow_ready, "mrow_ready", 1), "O": (o_read, "o_read", 1),
                "OT": (oT_ready, "oT_ready", 1), "h": (wo_read, "wo_read", 1), "wo": (wo_read, "wo_read", 1)}
        for g in range(3):
            READ[f"ct{g}"] = (ct_lo, "ct_lo", g + 1)
            READ[f"k{g}"] = (k_lo, "k_lo", g + 1)
            READ[f"v{g}"] = (v_ready, "v_ready", g + 1)
            READ[f"mk{g}"] = (mask_ready, "mask_ready", g + 1)

        def count_of(name, L, b, k):
            return START.get(name, 0) + B * sum(PER[name][:L]) + PER[name][L] * b + k

        scratch, products = {}, {}

        def upto(engine, name, L, b, k):
            if isinstance(b, int) or not PER[name][L]:
                return max(count_of(name, L, b if PER[name][L] else 0, k), 0)
            if engine not in scratch:
                scratch[engine] = [engine.alloc_register(f"count{i}") for i in range(4)]
                products[engine] = {}
            made, per = products[engine], PER[name][L]
            if per > 1 and (per not in made or made[per][1] is not b):
                product = made[per][0] if per in made else engine.alloc_register(f"times{per}")
                engine.reg_mul(product, b, per)
                made[per] = (product, b)
            if not count_of(name, L, 0, k):
                return made[per][0] if per > 1 else b
            scratch[engine].append(scratch[engine].pop(0))
            engine.reg_add(scratch[engine][-1], made[per][0] if per > 1 else b, count_of(name, L, 0, k))
            return scratch[engine][-1]

        def use(L, b, name):
            names = [n for n, _ in USES[L]]
            at = names.index(name)
            i = USES[L][at][1]
            return i, sum(bb == i for _, bb in USES[L][:at + 1])

        def width(L, g):
            if L == 2:
                return 0, S, S
            c = GROUPS[g][0]
            return COL[c], COL[c + 4] - COL[c], ROWS[c]

        def chunk(L, c):
            return (0, S) if L == 2 else (COL[c], ROWS[c])

        block = es.enter_context(nc.Block())

        @block.sync
        def _(sp):
            for dst, src in ((xall[:, :, :], x_in.rearrange("b s d -> s b d")),
                             (wq[:, :, :, :], w_qkv[:, :, 0:T * PARTS].rearrange("l c (t p) -> c l t p", t=T)),
                             (wk[:, :, :], w_qkv[:, :, T * PARTS:T * PARTS + D].rearrange("l c n -> c l n")),
                             (wv[:, :, :], w_qkv[:, :, T * PARTS + D:T * PARTS + 2 * D].rearrange("l c n -> c l n")),
                             (wo[:, :, :], w_o.rearrange("l c n -> c l n")), (w1[:, :], w_1),
                             (w2[:, :, :], w_2.rearrange("(j f) n -> f j n", f=128)),
                             (rows[:, :, :], rows_in), (cols[:, :], cols_in), (bq[:, :, :], bq_in),
                             (headmask[:, :], headmask_in), (ident[:, :], ident_in[0]),
                             (causal[:, :, :], causal_in)):
                sp.dma_start(dst, src).then_inc(const_in, 16)
            sp.dma_start(anymask[:, :], mask_in.rearrange("b o s k -> (b o s k)").rearrange("(p n) -> p n", p=128)
                         ).then_inc(mask_in_all, 16)

            def batch(L, b):
                if L == 1:
                    sp.dma_start(mask8[:, :], mask_in[bass.ds(b, 1), 0, :, :].rearrange("b s k -> (b s) k")
                                 ).then_inc(mask_loaded, 16)
                n_hi, n_lo = upto(sp, "k_hi", L, b, G[L]), upto(sp, "k_lo", L, b, G[L])
                n_read = upto(sp, "sexp_ready", L, b, 0)
                sp.wait_ge(k_hi, n_hi)
                sp.wait_ge(k_lo, n_lo)
                sp.wait_ge(sexp_ready, n_read)
                n = S if L == 2 else KEYS
                for t in range(T):
                    for j, part in enumerate((0, 0, 1)):
                        sp.dma_start(krep[32 * j:32 * j + 32, t, 0:n],
                                     kp[32 * t:32 * t + 32, part, 0:n]).then_inc(krep_in, 16)
                sp.wait_ge(mrow_ready, upto(sp, "mrow_ready", L, b, 1))
                sp.dma_start(qbd[PARTS:PARTS + 1, :, :, :].rearrange("o t h s -> o (t h) s"),
                             mrow[:, :]).then_inc(mrow_in, 16)
                if L == 3:
                    sp.wait_ge(out_ready, upto(sp, "out_ready", L, b, 1))
                    sp.dma_start(out[bass.ds(b, 1)].rearrange("b s d -> (b s) d"), outsb[:, :]).then_inc(out_sent, 16)

            for L in range(4):
                if L == 0:
                    batch(0, 0)
                with sp.Fori(int(L == 0), B) as b:
                    batch(L, b)
            sp.wait_ge(out_sent, 16 * B)

        @block.gpsimd
        def _(pool):
            pool.memset(half[:, :], -0.5).then_inc(pool_own, 1)
            pool.memset(vx[:, :, :, :], 0.0).then_inc(pool_own, 1)
            pool.wait_ge(pool_own, 2)
            pool.memset(vx[:, :, :, DH:DH + 1], 1.0).then_inc(const_ready, 1)

            def batch(L, b):
                pool.wait_ge(ct_hi, upto(pool, "ct_hi", L, b, 0))
                if L == 2:
                    pool.dma_start(nat[0:S, 0, :], ctx_in[bass.ds(b, 1), 0:S, :].rearrange("b s d -> (b s) d")
                                   ).then_inc(ctx_loaded, 16)
                else:
                    full = KEYS // NCH
                    pool.dma_start(nat[0:full, :, :], ctx_in[bass.ds(b, 1), 0:full * NCH, :].rearrange(
                        "b (p c) d -> (b p) c d", c=NCH)).then_inc(ctx_loaded, 16)
                    pool.dma_start(nat[full:full + 1, 0:LONG, :], ctx_in[bass.ds(b, 1), full * NCH:KEYS, :]
                                   ).then_inc(ctx_loaded, 16)
                if L == 0:
                    pool.wait_ge(ctx_loaded, upto(pool, "ctx_loaded", L, b, 32))
                    pool.tensor_tensor(sq[0:ROWS[0], 0:4, :], nat[0:ROWS[0], 0:4, :], nat[0:ROWS[0], 0:4, :], ALU.mult)
                    pool.tensor_tensor(sq[0:ROWS[4], 4:NCH, :], nat[0:ROWS[4], 4:NCH, :], nat[0:ROWS[4], 4:NCH, :],
                                       ALU.mult).then_inc(squares, 1)
                    pool.wait_ge(row_power, upto(pool, "row_power", L, b, 1))
                    pool.tensor_tensor(rinv[0:ROWS[0], 0:4], ssq[0:ROWS[0], 0:4], half[0:ROWS[0], 0:4], ALU.pow)
                    pool.tensor_tensor(rinv[0:ROWS[4], 4:NCH], ssq[0:ROWS[4], 4:NCH], half[0:ROWS[4], 4:NCH],
                                       ALU.pow).then_inc(pool_own, 1)
                    pool.wait_ge(pool_own, upto(pool, "pool_own", L, b, 1))
                    for c0, c1, r in ((0, 4, ROWS[0]), (4, NCH, ROWS[4])):
                        last = pool.tensor_tensor(nat[0:r, c0:c1, :], nat[0:r, c0:c1, :],
                                                  rinv[0:r, c0:c1].unsqueeze(2).broadcast_to([r, c1 - c0, D]), ALU.mult)
                    last.then_inc(ctx_normal, 1)
                pool.wait_ge(q_parts, upto(pool, "q_parts", L, b, 1))
                pool.wait_ge(sexp_ready, upto(pool, "sexp_ready", L, b, 0))
                for t in range(T):
                    last = pool.tensor_tensor(qbd[0:PARTS, t, :, :],
                                              qs[:, t, :].unsqueeze(1).broadcast_to([PARTS, HT, S]),
                                              headmask16[:, :].unsqueeze(2).broadcast_to([PARTS, HT, S]), ALU.mult)
                last.then_inc(q_spread, 1)
                if L:
                    pool.wait_ge(var_ready, upto(pool, "var_ready", L, b, 1))
                    pool.tensor_tensor(rstd[:, :], vare[:, :], half[0:S, 0:1], ALU.pow).then_inc(rstd_ready, 1)

            pool.wait_ge(x_power, 1)
            pool.tensor_tensor(rinv[0:S, 0:B], ssq[0:S, 0:B], half[0:S, 0:B], ALU.pow).then_inc(x_root, 1)
            pool.wait_ge(vector_ready, 1)
            for L in range(4):
                if L == 0:
                    batch(0, 0)
                with pool.Fori(int(L == 0), B) as b:
                    batch(L, b)

        @block.tensor
        def _(pe):
            def begin(L, b, name):
                names = [n for n, _ in USES[L]]
                i = USES[L][names.index(name)][1]
                mine = [n for n, bb in USES[L] if bb == i]
                at = mine.index(name)
                if at:
                    s, n, k = READ[mine[at - 1]]
                    pe.wait_ge(s, upto(pe, n, L, b, k))
                else:
                    s, n, k = READ[mine[-1]]
                    pe.wait_ge(s, upto(pe, n, L, b, 0))
                    if L:
                        s, n, k = READ[[n for n, bb in USES[L - 1] if bb == i][-1]]
                        pe.wait_ge(s, upto(pe, n, L, b if PER[n][L] else 0, 0))
                return bank[i], filled[i]

            def add_mask(ps, c, r, which):
                return pe.matmul(ps[0:r, 0:QW].rearrange("p (h s) -> p h s", h=HT), masked_by[0:r, which, 0:r],
                                 maskT[0:r, c, :].unsqueeze(1).broadcast_to([r, HT, S]), start=False, stop=True)

            def batch(L, b, masks=False):
                if L:
                    pe.wait_ge(ctx_loaded, upto(pe, "ctx_loaded", L, b, PER["ctx_loaded"][L]))
                else:
                    pe.wait_ge(ctx_normal, upto(pe, "ctx_normal", L, b, 1))
                for g in range(G[L]):
                    ps, done = begin(L, b, f"ct{g}")
                    c0, n, r = width(L, g)
                    for c in GROUPS[g] if L != 2 else [0]:
                        at = chunk(L, c)[0] - c0
                        last = pe.transpose(ps[:, at:at + r], nat[0:r, c, :], ident[0:r, 0:r])
                    last.then_inc(done, 1)
                for g in range(G[L]):
                    pe.wait_ge(ct_lo, upto(pe, "ct_lo", L, b, g + 1))
                    ps, done = begin(L, b, f"k{g}")
                    c0, n, r = width(L, g)
                    for j, (w, c) in enumerate(((0, 0), (0, 1), (1, 0))):
                        last = pe.matmul(ps[:, 0:n], wk16[:, w, L, :], ct[:, c, c0:c0 + n], start=(j == 0), stop=(j == 2))
                    last.then_inc(done, 1)
                for g in range(G[L]):
                    ps, done = begin(L, b, f"v{g}")
                    for i, c in enumerate(GROUPS[g] if L != 2 else [0]):
                        at, r = chunk(L, c)
                        for j, (w, p) in enumerate(((0, 0), (1, 0), (0, 1))):
                            last = pe.matmul(ps[0:r, D * i:D * i + D], ct[:, p, at:at + r], wv16[:, w, L, :],
                                             start=(j == 0), stop=(j == 2))
                    last.then_inc(done, 1)
                if L == 1:
                    pe.wait_ge(mask_scaled, upto(pe, "mask_scaled", L, b, 1))
                    for g in range(3):
                        ps, done = begin(L, b, f"mk{g}")
                        for i, c in enumerate(GROUPS[g]):
                            last = pe.transpose(ps[0:ROWS[c], :].bitcast(BF16)[:, S * i:S * i + S],
                                                maskb[:, c:c + NCH * (ROWS[c] - 1) + 1:NCH], identb[0:S, 0:S])
                        last.then_inc(done, 1)
                    pe.wait_ge(mask_ready, upto(pe, "mask_ready", L, b, 3))
                pe.wait_ge(x_copied, upto(pe, "x_copied", L, b, 1))
                ps, done = begin(L, b, "xT")
                pe.transpose(ps[:, 0:S], xcur[:, :], ident[0:S, 0:S]).then_inc(done, 1)
                pe.wait_ge(x_lo, upto(pe, "x_lo", L, b, 1))
                ps, done = begin(L, b, "q")
                for t in range(T):
                    for j, (w, p) in enumerate(((0, 0), (0, 1), (1, 0))):
                        last = pe.matmul(ps[0:PARTS, S * t:S * t + S], wq16[:, w, L, t, :], xT[:, p, :],
                                         start=(j == 0), stop=(j == 2))
                last.then_inc(done, 1)

                pe.wait_ge(krep_in, upto(pe, "krep_in", L, b, 16 * 12))
                pe.wait_ge(q_spread, upto(pe, "q_spread", L, b, 1))
                for c in CHUNKS[L]:
                    at, r = chunk(L, c)
                    for t in range(T):
                        j = T * c + t
                        pe.wait_ge(smax_used, upto(pe, "smax_used", L, b, max(j - SR + 1, 0)))
                        last = pe.matmul(smax[j % SR][0:r, 0:QW], krep[0:PARTS, t, at:at + r],
                                         qbd[0:PARTS, t, :, :].rearrange("p h s -> p (h s)"), start=True,
                                         stop=not masks)
                        if masks:
                            last = add_mask(smax[j % SR], c, r, 0)
                        last.then_inc(smax_ready, 1)
                n = S if L == 2 else ROWS[0]
                pe.wait_ge(smax_used, upto(pe, "smax_used", L, b, STEPS[L]))
                for i in range(2):
                    ps, done = begin(L, b, f"mt{i}")
                    for h in range(8):
                        last = pe.transpose(ps[0:S, :].bitcast(F16)[:, 128 * h:128 * h + n],
                                            mx[0:n, S * (8 * i + h):S * (8 * i + h) + S], ident16[0:n, 0:n])
                    last.then_inc(done, 1)
                pe.wait_ge(m_ready, upto(pe, "m_ready", L, b, 2))
                ps, done = begin(L, b, "mn")
                pe.transpose(ps[0:H, :].bitcast(F16)[:, 0:S], mneg[:, :], ident16[0:S, 0:S]).then_inc(done, 1)

                pe.wait_ge(mrow_in, upto(pe, "mrow_in", L, b, 16))
                pe.wait_ge(v_ready, upto(pe, "v_ready", L, b, G[L]))
                pe.wait_ge(acc_copied, upto(pe, "acc_copied", L, b, 0))
                steps = [(c, t) for c in CHUNKS[L] for t in range(T)]

                def values(j):
                    c, t = steps[j]
                    r = chunk(L, c)[1]
                    pe.wait_ge(probs_ready, upto(pe, "probs_ready", L, b, j + 1))
                    for i in range(HT):
                        last = pe.matmul(acc[32 * i:32 * i + VW, S * t:S * t + S], vx[0:r, c, HT * t + i, :],
                                         probs[0:r, j % PR, S * i:S * i + S], start=(j == 0), stop=(c == CHUNKS[L][-1]),
                                         skip_group_check=True)
                    last.then_inc(pv_done, 1)

                for j, (c, t) in enumerate(steps):
                    at, r = chunk(L, c)
                    if j >= SR:
                        pe.wait_ge(probs_ready, upto(pe, "probs_ready", L, b, j - SR + 1))
                    last = pe.matmul(sexp[j % SR][0:r, 0:QW], krep[:, t, at:at + r],
                                     qbd[:, t, :, :].rearrange("p h s -> p (h s)"), start=True, stop=not masks)
                    if masks:
                        last = add_mask(sexp[j % SR], c, r, 1)
                    last.then_inc(sexp_ready, 1)
                    if j >= SR - 1:
                        values(j - SR + 1)
                for j in range(STEPS[L] - SR + 1, STEPS[L]):
                    values(j)

                pe.wait_ge(acc_copied, upto(pe, "acc_copied", L, b, 1))
                ps, done = begin(L, b, "O")
                for t in range(T):
                    last = pe.transpose(ps[0:S, 128 * t:128 * t + 128], osb[:, S * t:S * t + S], ident[:, :])
                last.then_inc(done, 1)
                if L == 3:
                    return
                if L:
                    pe.wait_ge(o_normal, upto(pe, "o_normal", L, b, 1))
                else:
                    pe.wait_ge(o_read, upto(pe, "o_read", L, b, 1))
                ps, done = begin(L, b, "OT")
                pe.transpose(ps[:, 0:S], oatt[:, :], ident[0:S, 0:S]).then_inc(done, 1)
                pe.wait_ge(oT_ready, upto(pe, "oT_ready", L, b, 1))
                if L < 2:
                    ps, done = begin(L, b, "wo")
                    pe.matmul(ps[0:S, 0:D], oT[:, :], wo[:, L, :], start=True, stop=True).then_inc(done, 1)
                else:
                    ps, done = begin(L, b, "h")
                    for j in range(FF // 128):
                        last = pe.matmul(ps[:, S * j:S * j + S], w1[:, 128 * j:128 * j + 128], oT[:, :],
                                         start=True, stop=True)
                    last.then_inc(done, 1)
                    pe.wait_ge(h_ready, upto(pe, "h_ready", L, b, 4))
                    ps, done = begin(L, b, "wo")
                    for j in range(FF // 128):
                        last = pe.matmul(ps[0:S, 0:D], hT[:, j, :], w2[:, j, :], start=(j == 0), stop=(j == 3))
                    last.then_inc(done, 1)

            pe.wait_ge(const_ready, 2)
            pe.wait_ge(vector_ready, 1)
            batch(0, 0)
            with pe.Fori(1, B) as b:
                batch(0, b)
            ps = bank[0]
            pe.wait_ge(mask_counted, 1)
            pe.wait_ge(o_read, B)
            pe.matmul(acc[0:1, 0:1], maskcount[:, :], ones[:, :], start=True, stop=True).then_inc(mask_summed, 1)
            pe.wait_ge(flag_ready, 1)
            flag = pe.value_load(maskflag[0:1, 0:1])
            with pe.If(flag != 0):
                with pe.Fori(0, B) as b:
                    batch(1, b, masks=True)
            with pe.Else():
                with pe.Fori(0, B) as b:
                    batch(1, b)
            for L in (2, 3):
                with pe.Fori(0, B) as b:
                    batch(L, b)

        @block.scalar
        def _(act):
            def full(L, b, name):
                i, n = use(L, b, name)
                act.wait_ge(filled[i], upto(act, f"filled{i}", L, b, n))
                return bank[i]

            def batch(L, b):
                act.wait_ge(v_ready, upto(act, "v_ready", L, b, 0))
                for g in range(G[L]):
                    ps = full(L, b, f"ct{g}")
                    c0, n, _ = width(L, g)
                    if L:
                        op = act.copy(ct[:, 0, c0:c0 + n], ps[:, 0:n])
                    else:
                        op = act.mul(ct[:, 0, c0:c0 + n], ps[:, 0:n], cols[:, COLC["gkv"]:COLC["gkv"] + 1])
                    op.then_inc(ct_hi, 1)
                act.wait_ge(krep_in, upto(act, "krep_in", L, b, 0))
                for g in range(G[L]):
                    ps = full(L, b, f"k{g}")
                    c0, n, _ = width(L, g)
                    if L:
                        bk = COLC[f"bk{L}"]
                        op = act.activation(kp[:, 0, c0:c0 + n], ps[:, 0:n], ACT.Identity, bias=cols[:, bk:bk + 1])
                    else:
                        op = act.copy(kp[:, 0, c0:c0 + n], ps[:, 0:n])
                    op.then_inc(k_hi, 1)
                act.wait_ge(pv_done, upto(act, "pv_done", L, b, 0))
                for g in range(G[L]):
                    ps = full(L, b, f"v{g}")
                    r = width(L, g)[2]
                    c0, c1 = (0, 1) if L == 2 else (GROUPS[g][0], GROUPS[g][-1] + 1)
                    act.copy(vx[0:r, c0:c1, :, 0:DH], ps[0:r, 0:D * (c1 - c0)].rearrange(
                        "p (c h d) -> p c h d", h=H, d=DH)).then_inc(v_ready, 1)
                if L == 1:
                    act.wait_ge(mask_loaded, upto(act, "mask_loaded", L, b, 16))
                    act.copy(maskb[:, :], mask8[:, :]).then_inc(mask_scaled, 1)
                    act.wait_ge(probs_ready, upto(act, "probs_ready", L, b, 0))
                    for g in range(3):
                        ps = full(L, b, f"mk{g}")
                        c0, r = GROUPS[g][0], ROWS[GROUPS[g][0]]
                        act.copy(maskT[0:r, c0:c0 + 4, :], ps[0:r, :].bitcast(BF16)[:, 0:4 * S].rearrange(
                            "p (c s) -> p c s", c=4)).then_inc(mask_ready, 1)
                if L:
                    act.wait_ge(x_next, upto(act, "x_next", L - 1, b, 1))
                act.copy(xcur[:, :].rearrange("s (a d) -> s a d", a=1), xall[:, bass.ds(b, 1), :]).then_inc(x_copied, 1)
                ps = full(L, b, "xT")
                act.copy(xT[:, 0, :], ps[:, 0:S]).then_inc(x_hi, 1)
                ps = full(L, b, "mn")
                act.wait_ge(mrow_in, upto(act, "mrow_in", L, b, 0))
                act.copy(mrow[:, :], ps[0:H, :].bitcast(F16)[:, 0:S]).then_inc(mrow_ready, 1)
                for j in range(STEPS[L]):
                    r = chunk(L, j // T)[1]
                    if j < PR:
                        act.wait_ge(pv_done, upto(act, "pv_done", L, b, 0))
                    else:
                        act.wait_ge(pv_done, upto(act, "pv_done", L, b, j - PR + 1))
                    if L == 2:
                        act.wait_ge(masked_ready, upto(act, "masked_ready", L, b, j + 1))
                        src = masked[:, j % 2, :]
                    else:
                        act.wait_ge(sexp_ready, upto(act, "sexp_ready", L, b, j + 1))
                        src = sexp[j % SR][0:r, 0:QW]
                    act.activation(probs[0:r, j % PR, :], src, ACT.Exp).then_inc(probs_ready, 1)
                act.wait_ge(pv_done, upto(act, "pv_done", L, b, STEPS[L]))
                act.copy(osb[:, :], acc[:, 0:QW]).then_inc(acc_copied, 1)
                if L == 3:
                    return
                ps = full(L, b, "OT")
                act.copy(oT[:, :], ps[:, 0:S]).then_inc(oT_ready, 1)
                if L == 2:
                    ps = full(L, b, "h")
                    for j in range(FF // 128):
                        k = COLC["ffb0"] + j
                        act.activation(hT[:, j, :], ps[:, S * j:S * j + S], ACT.Gelu, bias=cols[:, k:k + 1]
                                       ).then_inc(h_ready, 1)

            act.wait_ge(const_ready, 2)
            act.wait_ge(vector_ready, 1)
            for L in range(4):
                if L == 0:
                    batch(0, 0)
                with act.Fori(int(L == 0), B) as b:
                    batch(L, b)
                if L == 0:
                    act.wait_ge(mask_in_all, 16)
                    act.activation(anymask[:, :], anymask[:, :], ACT.Copy, accum_out=maskcount[:, :]
                                   ).then_inc(mask_counted, 1)
                    act.wait_ge(mask_summed, 1)
                    act.copy(maskflag[:, :], acc[0:1, 0:1]).then_inc(flag_ready, 1)

        @block.vector
        def _(dve):
            count = [0]

            def full(L, b, name):
                i, n = use(L, b, name)
                dve.wait_ge(filled[i], upto(dve, f"filled{i}", L, b, n))
                return bank[i]

            def layernorm(L, b, own, src, dst, done):
                own(dve.tensor_reduce(mv[:, 0:1], src, AX, ALU.add))
                own(dve.scalar_tensor_tensor(out=xn[:, :], in0=mv[:, 0:1].broadcast_to([S, D]), scalar=-1.0 / D,
                                             in1=src, op0=ALU.mult, op1=ALU.add))
                own(dve.tensor_tensor_reduce(squared[:, :], xn[:, :], xn[:, :], 1.0, 0.0, ALU.mult, ALU.add,
                                             mv[:, 1:2]))
                dve.tensor_scalar(vare[:, :], mv[:, 1:2], 1.0 / D, EPS[L], ALU.mult, ALU.add).then_inc(var_ready, 1)
                dve.wait_ge(rstd_ready, upto(dve, "rstd_ready", L, b, 1))
                own(dve.scalar_tensor_tensor(out=xn[:, :], in0=xn[:, :], scalar=rstd[:, :],
                                             in1=rows[:, ROW[f"g{L}"], :], op0=ALU.mult, op1=ALU.mult))
                op = dve.tensor_tensor(dst, xn[:, :], rows[:, ROW[f"b{L}"], :], ALU.add)
                op.then_inc(done, 1)
                return op

            def batch(L, b):
                count[0] = 0

                def own(op):
                    count[0] += 1
                    op.then_inc(dve_own, 1)
                    dve.wait_ge(dve_own, upto(dve, "dve_own", L, b, count[0]))

                if L == 0:
                    dve.wait_ge(squares, upto(dve, "squares", L, b, 1))
                    for c0, c1, r in ((0, 4, ROWS[0]), (4, NCH, ROWS[4])):
                        op = dve.tensor_reduce(ssq[0:r, c0:c1], sq[0:r, c0:c1, :], AX, ALU.add)
                    own(op)
                    for c0, c1, r in ((0, 4, ROWS[0]), (4, NCH, ROWS[4])):
                        op = dve.tensor_scalar(ssq[0:r, c0:c1], ssq[0:r, c0:c1], 1.0 / D, EPS[0], ALU.mult, ALU.add)
                    op.then_inc(row_power, 1)
                for g in range(G[L]):
                    ps = full(L, b, f"ct{g}")
                    c0, n, _ = width(L, g)
                    dve.wait_ge(ct_hi, upto(dve, "ct_hi", L, b, g + 1))
                    if L:
                        op = dve.tensor_tensor(ct[:, 1, c0:c0 + n], ps[:, 0:n], ct[:, 0, c0:c0 + n], ALU.subtract)
                    else:
                        op = dve.scalar_tensor_tensor(out=ct[:, 1, c0:c0 + n], in0=ps[:, 0:n],
                                                      scalar=cols[:, COLC["gkv"]:COLC["gkv"] + 1],
                                                      in1=ct[:, 0, c0:c0 + n], op0=ALU.mult, op1=ALU.subtract)
                    op.then_inc(ct_lo, 1)
                for g in range(G[L]):
                    ps = full(L, b, f"k{g}")
                    c0, n, _ = width(L, g)
                    dve.wait_ge(k_hi, upto(dve, "k_hi", L, b, g + 1))
                    if L:
                        bk = COLC[f"bk{L}"]
                        op = dve.scalar_tensor_tensor(out=kp[:, 1, c0:c0 + n], in0=ps[:, 0:n], scalar=cols[:, bk:bk + 1],
                                                      in1=kp[:, 0, c0:c0 + n], op0=ALU.add, op1=ALU.subtract)
                    else:
                        op = dve.tensor_tensor(kp[:, 1, c0:c0 + n], ps[:, 0:n], kp[:, 0, c0:c0 + n], ALU.subtract)
                    op.then_inc(k_lo, 1)
                ps = full(L, b, "xT")
                dve.wait_ge(x_hi, upto(dve, "x_hi", L, b, 1))
                dve.tensor_tensor(xT[:, 1, :], ps[:, 0:S], xT[:, 0, :], ALU.subtract).then_inc(x_lo, 1)
                ps = full(L, b, "q")
                dve.scalar_tensor_tensor(out=qf[:, :, :], in0=ps[0:PARTS, 0:T * S].rearrange("p (t s) -> p t s", t=T),
                                         scalar=SCALE, in1=bqs[:, L, :].unsqueeze(2).broadcast_to([PARTS, T, S]),
                                         op0=ALU.mult, op1=ALU.add).then_inc(q_read, 1)
                dve.wait_ge(q_read, upto(dve, "q_read", L, b, 1))
                dve.wait_ge(q_spread, upto(dve, "q_spread", L, b, 0))
                own(dve.tensor_copy(qs[:, :, :], qf[:, :, :]))
                dve.tensor_tensor(qs[32:64, :, :], qf[32:64, :, :], qs[32:64, :, :], ALU.subtract).then_inc(q_parts, 1)

                for j in range(STEPS[L]):
                    c, t = divmod(j, T)
                    r = chunk(L, c)[1]
                    ps = smax[j % SR][0:r, 0:QW]
                    dst = mx[0:r, QW * t:QW * t + QW]
                    dve.wait_ge(smax_ready, upto(dve, "smax_ready", L, b, j + 1))
                    if L == 2:
                        v = "p (h s) -> p h s"
                        op = dve.tensor_tensor(dst.rearrange(v, h=HT), ps.rearrange(v, h=HT),
                                               causal[:, 0, :].unsqueeze(1).broadcast_to([S, HT, S]), ALU.add)
                    elif c == 0:
                        op = dve.tensor_copy(dst, ps)
                    else:
                        op = dve.tensor_tensor(dst, ps, dst, ALU.max)
                    op.then_inc(smax_used, 1)
                n = S if L == 2 else ROWS[0]
                for i in range(2):
                    ps = full(L, b, f"mt{i}")
                    dve.tensor_reduce(mneg[:, 8 * i:8 * i + 8],
                                      ps[0:S, :].bitcast(F16).rearrange("s (h n) -> s h n", h=8)[:, :, 0:n],
                                      AX, ALU.max, negate=True).then_inc(m_ready, 1)
                if L == 2:
                    for j in range(T):
                        dve.wait_ge(sexp_ready, upto(dve, "sexp_ready", L, b, j + 1))
                        dve.wait_ge(probs_ready, upto(dve, "probs_ready", L, b, j - 1 if j > 1 else 0))
                        v = "p (h s) -> p h s"
                        dve.tensor_tensor(masked[:, j % 2, :].rearrange(v, h=HT),
                                          sexp[j % SR][0:S, 0:QW].rearrange(v, h=HT),
                                          causal[:, 1, :].unsqueeze(1).broadcast_to([S, HT, S]), ALU.add
                                          ).then_inc(masked_ready, 1)

                ps = full(L, b, "O")
                o = ps[0:S, :].rearrange("s (h v) -> s h v", v=VW)
                own(dve.reciprocal(osum[:, :].unsqueeze(2), o[:, :, DH:DH + 1]))
                dve.tensor_tensor(oatt[:, :].rearrange("s (h d) -> s h d", h=H), o[:, :, 0:DH],
                                  osum[:, :].unsqueeze(2).broadcast_to([S, H, DH]), ALU.mult).then_inc(o_read, 1)
                dve.wait_ge(o_read, upto(dve, "o_read", L, b, 1))
                x = xall[:, bass.ds(b, 1), :].rearrange("s a d -> s (a d)")
                if L == 1:
                    dve.tensor_tensor(oatt[:, :], oatt[:, :], rows[:, ROW["bv1"], :], ALU.add).then_inc(o_normal, 1)
                if L < 2:
                    ps = full(L, b, "wo")
                    dve.tensor_tensor(y[:, :], ps[0:S, 0:D], rows[:, ROW[f"bo{L}"], :], ALU.add).then_inc(wo_read, 1)
                    dve.wait_ge(wo_read, upto(dve, "wo_read", L, b, 1))
                    if L == 0:
                        dve.tensor_tensor(x, y[:, :], x, ALU.add).then_inc(x_next, 1)
                    else:
                        own(dve.tensor_tensor(y[:, :], y[:, :], x, ALU.add))
                        layernorm(L, b, own, y[:, :], x, x_next)
                else:
                    own(dve.tensor_tensor(y[:, :], oatt[:, :], rows[:, ROW[f"bv{L}"], :], ALU.add))
                    own(dve.tensor_tensor(y[:, :], y[:, :], x, ALU.add))
                    if L == 3:
                        dve.wait_ge(out_sent, upto(dve, "out_sent", L, b, 0))
                        layernorm(L, b, own, y[:, :], outsb[:, :], out_ready)
                    else:
                        layernorm(L, b, own, y[:, :], oatt[:, :], o_normal)
                        dve.wait_ge(o_normal, upto(dve, "o_normal", L, b, 1))
                        ps = full(L, b, "wo")
                        dve.tensor_tensor(y[:, :], ps[0:S, 0:D], rows[:, ROW["ff2"], :], ALU.add).then_inc(wo_read, 1)
                        dve.wait_ge(wo_read, upto(dve, "wo_read", L, b, 1))
                        dve.tensor_tensor(x, y[:, :], oatt[:, :], ALU.add).then_inc(x_next, 1)
                OWNSEEN[L] = count[0]

            dve.wait_ge(const_in, 16 * 13)
            for w, parts in ((wq, wq16), (wk, wk16), (wv, wv16)):
                v = "p l t n -> p (l t n)" if w is wq else "p l n -> p (l n)"
                flat = w[tuple([slice(None)] * (4 if w is wq else 3))].rearrange(v)
                ax = parts[tuple([slice(None)] * (5 if w is wq else 4))]
                hi = ax[:, 0].rearrange(v)
                lo = ax[:, 1].rearrange(v)
                dve.tensor_copy(hi, flat).then_inc(setup, 1)
                count[0] += 1
                dve.wait_ge(setup, count[0])
                dve.tensor_tensor(lo, flat, hi, ALU.subtract)
            dve.memset(krep[PARTS:PARTS + 1, :, :], 1.0).then_inc(const_ready, 1)
            dve.tensor_copy(ident16[:, :], ident[:, :])
            dve.tensor_copy(identb[:, :], ident[:, :])
            for i in range(2):
                dve.tensor_scalar(masked_by[:, i, :], ident[:, :], MASKED[i], None, ALU.mult)
            dve.memset(ones[:, :], 1.0)
            dve.tensor_copy(headmask16[:, :], headmask[:, :])
            dve.tensor_scalar(bqs[:, :, :], bq[:, :, :], SCALE, None, ALU.mult)

            def step(op):
                count[0] += 1
                op.then_inc(setup, 1)
                dve.wait_ge(setup, count[0])

            step(dve.tensor_tensor(sq[0:S, 0:B, :], xall[:, :, :], xall[:, :, :], ALU.mult))
            step(dve.tensor_reduce(ssq[0:S, 0:B], sq[0:S, 0:B, :], AX, ALU.add))
            dve.tensor_scalar(ssq[0:S, 0:B], ssq[0:S, 0:B], 1.0 / D, EPS[0], ALU.mult, ALU.add).then_inc(x_power, 1)
            dve.wait_ge(x_root, 1)
            step(dve.tensor_tensor(xall[:, :, :], xall[:, :, :],
                                   rinv[0:S, 0:B].unsqueeze(2).broadcast_to([S, B, D]), ALU.mult))
            dve.tensor_tensor(xall[:, :, :], xall[:, :, :],
                              rows[:, ROW["gq"], :].unsqueeze(1).broadcast_to([S, B, D]), ALU.mult
                              ).then_inc(vector_ready, 1)
            dve.wait_ge(vector_ready, 1)
            for L in range(4):
                if L in (0, 3):
                    batch(L, 0)
                with dve.Fori(int(L in (0, 3)), B) as b:
                    batch(L, b)
            assert OWNSEEN == OWN, OWNSEEN


def kernel(**inputs):
    import concourse.bacc as _bacc
    from concourse.bass_utils import run_bass_kernel_spmd as _run

    a = {k: np.asarray(v) for k, v in inputs.items()}
    wq = np.stack([a["L0_xattn_wq"].T, a["L1_xattn_Wq"].T, a["L2_xattn_Wq"].T, a["L3_xattn_Wq"]])
    wk = np.stack([a["L0_xattn_wk"].T, a["L1_xattn_Wk"].T, a["L2_xattn_Wk"].T, a["L3_xattn_Wk"]])
    wv = np.stack([a["L0_xattn_wv"].T, a["L1_xattn_Wv"].T, a["L2_xattn_Wv"].T, a["L3_xattn_Wv"]])
    wq3 = np.concatenate([wq.reshape(4, D, T, 1, 32)] * 3, axis=3).reshape(4, D, T * PARTS)
    row = {"gq": "L0_xattn_gq", "bo0": "L0_xattn_bo", "bv1": "L1_xattn_bv", "bo1": "L1_xattn_bo",
           "g1": "L1_xattn_gamma", "b1": "L1_xattn_beta", "bv2": "L2_xattn_bv", "g2": "L2_xattn_ln_g",
           "b2": "L2_xattn_ln_b", "ff2": "L2_xattn_b2", "bv3": "L3_xattn_bv", "g3": "L3_xattn_ln_gamma",
           "b3": "L3_xattn_ln_beta"}
    rows = np.stack([a[row[n]] for n in ROW])
    b1 = a["L2_xattn_b1"].reshape(FF // 128, 128)
    cols = np.stack([a["L0_xattn_gkv"], a["L1_xattn_bk"], a["L2_xattn_bk"], a["L3_xattn_bk"], *b1], axis=1)
    zero = np.zeros(D, np.float32)
    bq = np.stack([zero, a["L1_xattn_bq"], a["L2_xattn_bq"], a["L3_xattn_bq"]]).reshape(4, T, 1, 32)
    bq = np.concatenate([bq] * 3, axis=2).reshape(4, T, PARTS).transpose(2, 0, 1)
    headmask = np.zeros((PARTS, HT), np.float32)
    for p in range(PARTS):
        headmask[p, p % 32 // DH] = 1.0
    later = np.arange(S)[:, None] > np.arange(S)[None, :]
    causal = np.zeros((S, 2, S), np.float32)
    causal[:, 0][later] = -30000.0
    causal[:, 1][later] = -1e9
    arrays = {
        "ctx": a["ctx_1024"], "x": a["x"], "mask": a["mask_Bx1xSxS2_bf0"], "w_qkv": np.concatenate([wq3, wk, wv], axis=2),
        "w_o": np.stack([a["L0_xattn_wo"].T, a["L1_xattn_Wo"].T]), "w_1": a["L2_xattn_W1"].T, "w_2": a["L2_xattn_W2"].T,
        "rows": np.broadcast_to(rows, (S,) + rows.shape), "cols": cols, "bq": bq, "headmask": headmask,
        "ident": np.eye(128, dtype=np.float32)[None], "causal": causal,
    }
    nc = _bacc.Bacc("TRN2", target_bir_lowering=False, num_devices=1)
    args = []
    for name, value in arrays.items():
        arrays[name] = np.ascontiguousarray(value)
        args.append(nc.dram_tensor(f"in_{name}", value.shape, U8 if name == "mask" else F32, kind="ExternalInput").ap())
    out = nc.dram_tensor("out_0", (B, S, D), F32, kind="ExternalOutput").ap()
    build(nc, *args, out)
    r = _run(nc, [{f"in_{k}": v for k, v in arrays.items()}], core_ids=[0])
    return r.results[0]["out_0"]
```

```python
from contextlib import ExitStack

import numpy as np

import concourse.bass as bass
from concourse import mybir

F32 = mybir.dt.float32
F16 = mybir.dt.float16
BF16 = mybir.dt.bfloat16
U8 = mybir.dt.uint8
I32 = mybir.dt.int32
ALU = mybir.AluOpType
ACT = mybir.ActivationFunctionType
AX = mybir.AxisListType.X

B, S, D = 8, 100, 128
KEYS = 1444
H, DH = 16, 8
T, HT = 4, 4
QW = HT * S
FF = 512
NCH = 12
LONG = KEYS - (KEYS // NCH) * NCH
ROWS = [KEYS // NCH + (c < LONG) for c in range(NCH)]
COL = [sum(ROWS[:c]) for c in range(NCH + 1)]
GROUPS = [range(0, 4), range(4, 8), range(8, 12)]
SCALE = float(DH) ** -0.5
MASKED = [-30000.0, -1e30]
VW = 32
PAIRS = H // 2
PR, SR = 6, 2
PARTS = 3 * 32

ROW = {n: i for i, n in enumerate(
    ["gq", "bo0", "bv1", "bo1", "g1", "b1", "bv2", "g2", "b2", "ff2", "bv3", "g3", "b3"])}
COLC = {n: i for i, n in enumerate(["gkv", "bk1", "bk2", "bk3", "ffb0", "ffb1", "ffb2", "ffb3"])}

USES2 = [("ct0", 0), ("k0", 1), ("v0", 2), ("xT", 0), ("q", 1), ("mt0", 0), ("mt1", 1), ("mn", 2), ("O", 0),
         ("OT", 1), ("h", 2), ("wo", 0)]
CHUNKS = [range(NCH), range(NCH), range(1), range(NCH)]
STEPS = [T * len(c) for c in CHUNKS]
OWN = [4, 6, 8, 7]
EPS = [1e-6, 1e-5, 1e-5, 1e-6]

NSTEP = NCH * T
AT = {"ct0": 0, "ct1": 2, "ct2": 4, "O": 5, "k0": 8, "OT": 9, "k1": 11, "wo": 12, "k2": 14, "xT": 16, "q": 18,
      "v0": 21, "v1": 23, "v2": 25, "mk0": 27, "mk1": 29, "mk2": 31, "mn": 43}
PVLAG = 3
VALUES_AT = [5, 5, 6, 6] + [j + PVLAG for j in range(4, NSTEP)]
NPAIR = NSTEP // 2
MAX_AT = [i * 40 // NPAIR for i in range(NPAIR)]
MT_AT = 40
ACC_AT = 3


class Unit:
    def __init__(self, layer, batch, reg=None, parity=None):
        self.L, self.batch, self.reg = layer, batch, reg
        self.par = batch % 2 if parity is None else parity

    def rows_of(self, tile):
        if self.reg is None:
            return tile[:, self.batch, :]
        return tile[:, bass.ds(self.reg + self.batch if self.batch else self.reg, 1), :].rearrange("s a d -> s (a d)")




def build(nc, ctx_in, x_in, mask_in, w_qkv, w_o, w_1, w_2, rows_in, cols_in, bq_in, headmask_in, ident_in, causal_in, out):
    with ExitStack() as es:
        def sb(name, shape, dt=F32):
            return es.enter_context(nc.sbuf_tensor(name, shape, dt))

        def psum(name, banks=1):
            return es.enter_context(nc.psum_tensor(name, [128, 512 * banks], F32))

        wq = sb("wq", [128, 4, T, PARTS])
        wk = sb("wk", [128, 4, D])
        wv = sb("wv", [128, 4, D])
        wo = sb("wo", [128, 2, D])
        w1 = sb("w1", [128, FF])
        w2 = sb("w2", [128, FF // 128, D])
        wq16 = sb("wq16", [128, 2, 4, T, PARTS], F16)
        wk16 = sb("wk16", [128, 2, 4, D], F16)
        wv16 = sb("wv16", [128, 2, 4, D], F16)
        rows = sb("rows", [S, len(ROW), D])
        cols = sb("cols", [128, len(COLC)])
        bq = sb("bq", [PARTS, 4, T])
        bqs = sb("bqs", [PARTS, 4, T])
        headmask = sb("headmask", [PARTS, HT])
        headmask16 = sb("headmask16", [PARTS, HT], F16)
        ident = sb("ident", [128, 128])
        ident16 = sb("ident16", [128, 128], F16)
        identb = sb("identb", [128, 128], BF16)
        masked_by = sb("masked_by", [128, 2, 128], BF16)
        causal = sb("causal", [S, 2, S])
        half = sb("half", [128, NCH])
        ones = sb("ones", [128, 1])
        anymask = sb("anymask", [128, B * S * KEYS // 128], U8)
        maskcount = sb("maskcount", [128, 1])
        maskflag = sb("maskflag", [1, 1], I32)
        xall = sb("xall", [S, B, D])
        mask8 = sb("mask8", [S, KEYS], U8)
        maskb = sb("maskb", [S, KEYS], BF16)
        maskmax = sb("maskmax", [128, 2, NCH, S], BF16)
        maskexp = sb("maskexp", [128, 2, NCH, S], BF16)
        nat = sb("nat", [128, NCH, D])
        sq = sb("sq", [128, NCH, D])
        ssq = sb("ssq", [128, NCH])
        rinv = sb("rinv", [128, NCH])
        ctf = sb("ctf", [128, KEYS])
        ct = sb("ct", [128, 2, 2, KEYS], F16)
        kf = sb("kf", [128, KEYS])
        kp = sb("kp", [128, 2, KEYS], F16)
        krep = sb("krep", [PARTS + 1, 2, T, KEYS], F16)
        vx = sb("vx", [128, 2, NCH * PAIRS, VW])
        xcur = sb("xcur", [S, D])
        xT = sb("xT", [128, 2, S], F16)
        qf = sb("qf", [PARTS, T, S])
        qs = sb("qs", [PARTS, T, S], F16)
        qmax = sb("qmax", [PARTS, 2, T, HT, S], F16)
        qexp = sb("qexp", [PARTS + 1, 2, T, HT, S], F16)
        mx = sb("mx", [128, T * QW], F16)
        mneg = sb("mneg", [S, H], F16)
        mrow = sb("mrow", [H, S], F16)
        masked = sb("masked", [S, 2, QW])
        probs = sb("probs", [128, PR, QW])
        osb = sb("osb", [128, QW])
        osum = sb("osum", [S, H])
        oatt = sb("oatt", [S, D])
        oT = sb("oT", [128, S])
        y = sb("y", [S, D])
        squared = sb("squared", [S, D])
        mv = sb("mv", [S, 2])
        vare = sb("vare", [S, 1])
        rstd = sb("rstd", [S, 1])
        xn = sb("xn", [S, D])
        hT = sb("hT", [128, FF // 128, S])
        outsb = sb("outsb", [S, D])

        smax = [psum(f"smax{i}", 2) for i in range(SR)]
        sexp = [psum(f"sexp{i}") for i in range(SR)]
        acc = psum("acc")
        shared = psum("shared")

        G = [3, 3, 1, 3]
        one, no2 = [1] * 4, [1, 1, 1, 0]
        PER = {
            "ctx_loaded": [32, 32, 16, 32], "row_power": [1, 0, 0, 0], "ctx_normal": [1, 0, 0, 0],
            "ct_filled": G, "ct_read": G, "ct_lo": G, "k_filled": G, "k_read": G, "k_lo": G,
            "krep_in0": [16 * 12] * 4, "krep_in1": [192, 192, 0, 192], "krep_in2": [192, 192, 0, 192],
            "x_copied": one, "xT_filled": one, "x_hi": one, "x_lo": one, "q_filled": one, "q_read": one,
            "q_parts": one, "q_spread": one, "qexp_in": [16] * 4, "v_filled": G, "v_ready": G,
            "mask_loaded": [0, 16, 0, 0], "mask_copied": [0, 1, 0, 0], "mk_filled": [0, 3, 0, 0],
            "mask_ready": [0, 3, 0, 0], "maskexp_in": [0, 32, 0, 0],
            "smax_ready": [s // 2 for s in STEPS], "smax_used": [s // 2 for s in STEPS], "mt_filled": [2] * 4,
            "m_ready": [2] * 4, "mn_filled": one, "mrow_ready": one, "mrow_in": [16] * 4,
            "sexp_ready": STEPS, "masked_ready": [0, 0, 4, 0], "probs_ready": STEPS, "pv_done": STEPS,
            "acc_copied": one, "o_filled": one, "o_read": one, "o_normal": [0, 1, 1, 0], "oT_filled": no2,
            "oT_ready": no2, "h_filled": [0, 0, 1, 0], "h_ready": [0, 0, 4, 0], "wo_filled": no2, "wo_read": no2,
            "var_ready": [0, 1, 1, 1], "rstd_ready": [0, 1, 1, 1], "x_next": no2, "out_ready": [0, 0, 0, 1],
            "out_sent": [0, 0, 0, 16],
            "own_power": [2, 0, 0, 0], "own_q": one, "own_o": [1, 1, 1, 3], "own_y": [0, 1, 2, 0],
            "own_ln": [0, 4, 4, 4], "own_rinv": [1, 0, 0, 0],
        }
        setup_names = ["const_in", "pool_ready", "const_ready", "x_power", "x_root", "vector_ready", "setup",
                       "mask_in_all", "mask_counted", "flag_filled", "flag_ready"]
        sem = {name: es.enter_context(nc.semaphore(name)) for name in list(PER) + setup_names}
        READ = {"xT": ("x_lo", 1), "q": ("q_read", 1), "mn": ("mrow_ready", 1), "O": ("o_read", 1),
                "OT": ("oT_ready", 1), "h": ("h_ready", 4), "wo": ("wo_read", 1), "flag": ("flag_ready", 1)}
        for g in range(3):
            READ[f"ct{g}"] = ("ct_read", g + 1)
            READ[f"k{g}"] = ("k_read", g + 1)
            READ[f"v{g}"] = ("v_ready", g + 1)
            READ[f"mk{g}"] = ("mask_ready", g + 1)

        registers = {}

        def at(engine, name, u, k):
            per = PER[name][u.L]
            value = B * sum(PER[name][:u.L]) + per * u.batch + k
            if u.reg is None or not per:
                return sem[name], max(value, 0)
            if engine not in registers:
                registers[engine] = ([engine.alloc_register(f"count{i}") for i in range(4)], {})
            counts, products = registers[engine]
            if per > 1 and (per not in products or products[per][1] is not u.reg):
                product = products[per][0] if per in products else engine.alloc_register(f"times{per}")
                engine.reg_mul(product, u.reg, per)
                products[per] = (product, u.reg)
            term = products[per][0] if per > 1 else u.reg
            if value == 0:
                return sem[name], term
            counts.append(counts.pop(0))
            engine.reg_add(counts[-1], term, value)
            return sem[name], counts[-1]

        def groups(u):
            if u.L == 2:
                return [([0], 0, S, S)]
            return [(list(g), COL[g[0]], COL[g[-1] + 1] - COL[g[0]], ROWS[g[0]]) for g in GROUPS]

        def chunk(u, c):
            return (0, S) if u.L == 2 else (COL[c], ROWS[c])

        class Stage:
            def __init__(self, load=None, prep=None, top=None, exp=None, post=None):
                self.load, self.prep, self.top, self.exp, self.post = load, prep, top, exp, post

        def stage_of(n, units, reg=None, base=0):
            def unit(i):
                if not 0 <= i < len(units):
                    return None
                u = units[i]
                if reg is None:
                    return u
                return Unit(u.L, u.batch - units[base].batch, reg, u.par)
            return Stage(unit(n + 3), unit(n + 2), unit(n + 1), unit(n), unit(n - 1))

        def pipeline(engine, units, run, tail=None, first=-3, last=None):
            n = first
            last = len(units) if last is None else last
            while n <= last:
                b0 = units[n].batch if 0 <= n < len(units) else None
                if b0 == 1 and n + 3 <= last:
                    with engine.Fori(1, 4, 2) as b:
                        enter_loop(n, units, b)
                        run(stage_of(n, units, b, n), n)
                        run(stage_of(n + 1, units, b, n), n)
                        leave_loop(n, units, b)
                    n += 4
                else:
                    run(stage_of(n, units), n)
                    n += 1

        held = [None]

        def enter_loop(n, units, b):
            if held[0] is not None:
                use, u = held[0]
                if use == "mn" and u.reg is None:
                    held[0] = ("mn", Unit(u.L, u.batch - units[n].batch, b, u.par))

        def leave_loop(n, units, b):
            if held[0] is not None and held[0][1].reg is not None:
                use, u = held[0]
                held[0] = (use, Unit(u.L, u.batch + units[n + 2].batch, None, u.par))

        ALL = [Unit(0, b) for b in range(B)] + [Unit(1, b) for b in range(B)]
        LAST = [Unit(3, b) for b in range(B)]
        FLAG_STAGE = 0
        MASK_STAGE = B - 1

        block = es.enter_context(nc.Block())

        @block.sync
        def _(sp):
            for dst, src in ((ident[:, :], ident_in[0]), (xall[:, :, :], x_in.rearrange("b s d -> s b d")),
                             (rows[:, :, :], rows_in), (cols[:, :], cols_in),
                             (wk[:, :, :], w_qkv[:, :, T * PARTS:T * PARTS + D].rearrange("l c n -> c l n")),
                             (wq[:, :, :, :], w_qkv[:, :, 0:T * PARTS].rearrange("l c (t p) -> c l t p", t=T)),
                             (wv[:, :, :], w_qkv[:, :, T * PARTS + D:T * PARTS + 2 * D].rearrange("l c n -> c l n")),
                             (wo[:, :, :], w_o.rearrange("l c n -> c l n")), (w1[:, :], w_1),
                             (w2[:, :, :], w_2.rearrange("(j f) n -> f j n", f=128)),
                             (bq[:, :, :], bq_in), (headmask[:, :], headmask_in), (causal[:, :, :], causal_in)):
                sp.dma_start(dst, src).then_inc(sem["const_in"], 16)

            def batch_of(array, u):
                size = int(np.prod(array.shape[1:]))
                flat = array.rearrange(" ".join("abcd"[:len(array.shape)]) + " -> (" + " ".join(
                    "abcd"[:len(array.shape)]) + ")")
                start = u.batch if u.reg is None else u.reg + u.batch
                return flat[bass.ds(start * size, size)]

            def wait_alone(count, u):
                if u.reg is not None:
                    sp.wait_ge(sem["const_in"], 16 * 13)
                sp.wait_ge(*count)

            def load(u):
                src = batch_of(ctx_in, u)
                count = at(sp, "ct_filled", u, 0)
                wait_alone(count, u)
                if u.L == 2:
                    sp.dma_start(nat[0:S, 0, :], src[0:S * D].rearrange("(s d) -> s d", d=D)
                                 ).then_inc(sem["ctx_loaded"], 16)
                    return
                full = KEYS // NCH
                sp.dma_start(nat[0:full, :, :], src[0:full * NCH * D].rearrange("(p c d) -> p c d", c=NCH, d=D)).then_inc(sem["ctx_loaded"], 16)
                sp.dma_start(nat[full:full + 1, 0:LONG, :], src[full * NCH * D:KEYS * D].rearrange("(b c d) -> b c d", b=1, d=D)
                             ).then_inc(sem["ctx_loaded"], 16)

            def replicate(u, g, before, steps):
                _, c0, n, _ = groups(u)[g]
                counts = [at(sp, "k_lo", u, g + 1)]
                if before is not None:
                    counts.append(at(sp, "sexp_ready", before, steps))
                for count in counts:
                    sp.wait_ge(*count)
                for t in range(T):
                    for j, part in enumerate((0, 0, 1)):
                        sp.dma_start(krep[32 * j:32 * j + 32, u.par, t, c0:c0 + n],
                                     kp[32 * t:32 * t + 32, part, c0:c0 + n]).then_inc(sem[f"krep_in{g}"], 16)

            def exp_copies(u, before):
                counts = [at(sp, "q_spread", u, 1)]
                if before is not None:
                    counts.append(at(sp, "sexp_ready", before, 1))
                for count in counts:
                    sp.wait_ge(*count)
                sp.dma_start(qexp[0:PARTS, u.par, :, :, :].rearrange("p t h s -> p (t h s)"),
                             qmax[:, u.par, :, :, :].rearrange("p t h s -> p (t h s)")).then_inc(sem["qexp_in"], 16)
                if u.L == 1:
                    sp.wait_ge(*at(sp, "mask_ready", u, 3))
                    full = KEYS // NCH
                    sp.dma_start(maskexp[0:full, u.par, :, :], maskmax[0:full, u.par, :, :]
                                 ).then_inc(sem["maskexp_in"], 16)
                    sp.dma_start(maskexp[full:full + 1, u.par, 0:LONG, :], maskmax[full:full + 1, u.par, 0:LONG, :]
                                 ).then_inc(sem["maskexp_in"], 16)

            def maximum_row(u):
                sp.wait_ge(*at(sp, "mrow_ready", u, 1))
                sp.dma_start(qexp[PARTS:PARTS + 1, u.par, :, :, :].rearrange("o t h s -> o (t h) s"), mrow[:, :]
                             ).then_inc(sem["mrow_in"], 16)

            def store(u):
                dst = batch_of(out, u)
                count = at(sp, "out_ready", u, 1)
                wait_alone(count, u)
                sp.dma_start(dst.rearrange("(s d) -> s d", d=D), outsb[:, :]
                             ).then_inc(sem["out_sent"], 16)

            def stage(s, n):
                if s.top is not None:
                    replicate(s.top, 2, s.post, NSTEP)
                    exp_copies(s.top, s.exp)
                if s.prep is not None and s.prep.L == 1:
                    src = batch_of(mask_in, s.prep)
                    count = at(sp, "mask_copied", s.prep, 0)
                    wait_alone(count, s.prep)
                    sp.dma_start(mask8[:, :], src.rearrange("(s k) -> s k", k=KEYS)
                                 ).then_inc(sem["mask_loaded"], 16)
                if s.load is not None:
                    load(s.load)
                if s.prep is not None:
                    replicate(s.prep, 0, s.exp, NSTEP // 3)
                if s.post is not None and s.post.L == 3:
                    store(s.post)
                if s.prep is not None:
                    replicate(s.prep, 1, s.exp, 2 * NSTEP // 3)
                if s.top is not None:
                    maximum_row(s.top)

            sp_started = [False]

            def run(s, n):
                stage(s, n)
                if not sp_started[0]:
                    sp_started[0] = True
                    sp.dma_start(anymask[:, :], mask_in.rearrange("b o s k -> (b o s k)").rearrange(
                        "(p n) -> p n", p=128)).then_inc(sem["mask_in_all"], 16)

            pipeline(sp, ALL, run)
            with sp.Fori(1, B + 1) as b:
                u = Unit(2, -1, b, 0)
                load(u)
                replicate(u, 0, u, 0)
                exp_copies(u, None)
                maximum_row(u)
            pipeline(sp, LAST, stage)
            sp.wait_ge(sem["out_sent"], 16 * B)

        @block.gpsimd
        def _(pool):
            def low_part(u, g, src, dst, reads, done):
                _, c0, n, _ = groups(u)[g]
                pool.wait_ge(*at(pool, reads, u, g + 1))
                pool.tensor_tensor(dst[:, 1, c0:c0 + n], src[:, c0:c0 + n], dst[:, 0, c0:c0 + n], ALU.subtract
                                   ).then_inc(sem[done], 1)

            def root(u):
                pool.wait_ge(*at(pool, "var_ready", u, 1))
                pool.tensor_tensor(rstd[:, :], vare[:, :], half[0:S, 0:1], ALU.pow).then_inc(sem["rstd_ready"], 1)

            def spread(u, before):
                if before is not None:
                    pool.wait_ge(*at(pool, "smax_used", before, 0))
                    pool.wait_ge(*at(pool, "qexp_in", before, 0))
                pool.wait_ge(*at(pool, "q_parts", u, 1))
                for t in range(T):
                    last = pool.tensor_tensor(qmax[:, u.par, t, :, :],
                                              qs[:, t, :].unsqueeze(1).broadcast_to([PARTS, HT, S]),
                                              headmask16[:, :].unsqueeze(2).broadcast_to([PARTS, HT, S]), ALU.mult)
                last.then_inc(sem["q_spread"], 1)

            def normalise(u):
                pool.wait_ge(*at(pool, "row_power", u, 1))
                for c0, c1, r in ((0, 4, ROWS[0]), (4, NCH, ROWS[4])):
                    last = pool.tensor_tensor(rinv[0:r, c0:c1], ssq[0:r, c0:c1], half[0:r, c0:c1], ALU.pow)
                last.then_inc(sem["own_rinv"], 1)
                pool.wait_ge(*at(pool, "own_rinv", u, 1))
                for c0, c1, r in ((0, 4, ROWS[0]), (4, NCH, ROWS[4])):
                    last = pool.tensor_tensor(nat[0:r, c0:c1, :], nat[0:r, c0:c1, :],
                                              rinv[0:r, c0:c1].unsqueeze(2).broadcast_to([r, c1 - c0, D]), ALU.mult)
                last.then_inc(sem["ctx_normal"], 1)

            def parts(u):
                for g in range(G[u.L]):
                    low_part(u, g, ctf, ct[:, u.par], "ct_read", "ct_lo")
                for g in range(G[u.L]):
                    low_part(u, g, kf, kp, "k_read", "k_lo")

            def stage(s, n):
                if s.prep is not None:
                    parts(s.prep)
                if s.post is not None and s.post.L:
                    root(s.post)
                if s.prep is not None:
                    spread(s.prep, s.top)
                if s.load is not None and s.load.L == 0:
                    normalise(s.load)

            pool.memset(half[:, :], -0.5).then_inc(sem["pool_ready"], 1)
            for i in range(2):
                pool.memset(vx[:, i, :, :], 0.0).then_inc(sem["pool_ready"], 1)
                pool.wait_ge(sem["pool_ready"], 2 + 2 * i)
                pool.memset(vx[:, i, :, 0:2 * (DH + 1)].rearrange("p a (f e) -> p a f e", f=2)[:, :, :, DH:DH + 1], 1.0
                            ).then_inc(sem["pool_ready"], 1)
                pool.wait_ge(sem["pool_ready"], 3 + 2 * i)
            pool.wait_ge(sem["x_power"], 1)
            pool.tensor_tensor(rinv[0:S, 0:B], ssq[0:S, 0:B], half[0:S, 0:B], ALU.pow).then_inc(sem["x_root"], 1)
            pool.wait_ge(sem["vector_ready"], 1)
            pipeline(pool, ALL, stage)
            with pool.Fori(1, B + 1) as b:
                u = Unit(2, -1, b, 0)
                parts(u)
                spread(u, u)
                root(u)
            pipeline(pool, LAST, stage)

        @block.tensor
        def _(pe):
            def begin(use, u):
                if held[0] is not None:
                    before, v = held[0]
                    if before == "flag":
                        pe.wait_ge(sem["flag_ready"], 1)
                    else:
                        pe.wait_ge(*at(pe, READ[before][0], v, READ[before][1]))
                held[0] = (use, u)
                return shared

            def context(u, g):
                if g == 0:
                    pe.wait_ge(*at(pe, "ctx_normal", u, 1) if u.L == 0 else
                               at(pe, "ctx_loaded", u, PER["ctx_loaded"][u.L]))
                ps = begin(f"ct{g}", u)
                chunks, c0, _, r = groups(u)[g]
                for c in chunks:
                    to = chunk(u, c)[0] - c0
                    last = pe.transpose(ps[:, to:to + r], nat[0:r, c, :], ident[0:r, 0:r])
                last.then_inc(sem["ct_filled"], 1)

            def keys(u, g):
                pe.wait_ge(*at(pe, "ct_lo", u, g + 1))
                ps = begin(f"k{g}", u)
                _, c0, n, _ = groups(u)[g]
                for j, (w, c) in enumerate(((0, 0), (0, 1), (1, 0))):
                    last = pe.matmul(ps[:, 0:n], wk16[:, w, u.L, :], ct[:, u.par, c, c0:c0 + n], start=(j == 0),
                                     stop=(j == 2))
                last.then_inc(sem["k_filled"], 1)

            def vals(u, g):
                ps = begin(f"v{g}", u)
                for i, c in enumerate(groups(u)[g][0]):
                    c0, r = chunk(u, c)
                    for j, (w, p) in enumerate(((0, 0), (1, 0), (0, 1))):
                        last = pe.matmul(ps[0:r, D * i:D * i + D], ct[:, u.par, p, c0:c0 + r], wv16[:, w, u.L, :],
                                         start=(j == 0), stop=(j == 2))
                last.then_inc(sem["v_filled"], 1)

            def mask(u, g):
                if g == 0:
                    pe.wait_ge(*at(pe, "mask_copied", u, 1))
                ps = begin(f"mk{g}", u)
                for i, c in enumerate(GROUPS[g]):
                    last = pe.transpose(ps[0:ROWS[c], :].bitcast(BF16)[:, S * i:S * i + S],
                                        maskb[:, c:c + NCH * (ROWS[c] - 1) + 1:NCH], identb[0:S, 0:S])
                last.then_inc(sem["mk_filled"], 1)

            def inputs(u):
                pe.wait_ge(*at(pe, "x_copied", u, 1))
                ps = begin("xT", u)
                pe.transpose(ps[:, 0:S], xcur[:, :], ident[0:S, 0:S]).then_inc(sem["xT_filled"], 1)

            def queries(u):
                pe.wait_ge(*at(pe, "x_lo", u, 1))
                ps = begin("q", u)
                for t in range(T):
                    for j, (w, p) in enumerate(((0, 0), (0, 1), (1, 0))):
                        last = pe.matmul(ps[0:PARTS, S * t:S * t + S], wq16[:, w, u.L, t, :], xT[:, p, :],
                                         start=(j == 0), stop=(j == 2))
                last.then_inc(sem["q_filled"], 1)

            def add_mask(ps, tile, which, c, r):
                return pe.matmul(ps.rearrange("p (h s) -> p h s", h=HT), masked_by[0:r, which, 0:r],
                                 tile[0:r, c, :].unsqueeze(1).broadcast_to([r, HT, S]), start=False, stop=True)

            def max_scores(u, i, masks):
                c, t = divmod(2 * i, T)
                c0, r = chunk(u, c)
                if i == 0:
                    pe.wait_ge(*at(pe, "q_spread", u, 1))
                    pe.wait_ge(*at(pe, "m_ready", u, 0))
                    if masks:
                        pe.wait_ge(*at(pe, "mask_ready", u, 3))
                if c % 4 == 0 and t == 0:
                    pe.wait_ge(*at(pe, f"krep_in{c // 4}", u, 16 * 12))
                pe.wait_ge(*at(pe, "smax_used", u, i - 1))
                for k in range(2):
                    ps = smax[i % SR][0:r, 512 * k:512 * k + QW]
                    last = pe.matmul(ps, krep[0:PARTS, u.par, t + k, c0:c0 + r],
                                     qmax[:, u.par, t + k, :, :].rearrange("p h s -> p (h s)"), start=True, stop=not masks)
                    if masks:
                        last = add_mask(ps, maskmax[:, u.par], 0, c, r)
                last.then_inc(sem["smax_ready"], 1)

            def maxima(u):
                n = chunk(u, 0)[1]
                pe.wait_ge(*at(pe, "smax_used", u, STEPS[u.L] // 2))
                for i in range(2):
                    for h in range(8):
                        last = pe.transpose(smax[0][0:S, 512 * i:512 * i + 512].bitcast(F16)[:, 128 * h:128 * h + n],
                                            mx[0:n, S * (8 * i + h):S * (8 * i + h) + S], ident16[0:n, 0:n])
                    last.then_inc(sem["mt_filled"], 1)

            def maximum_rows(u):
                pe.wait_ge(*at(pe, "m_ready", u, 2))
                ps = begin("mn", u)
                pe.transpose(ps[0:H, :].bitcast(F16)[:, 0:S], mneg[:, :], ident16[0:S, 0:S]
                             ).then_inc(sem["mn_filled"], 1)

            def exp_scores(u, j, masks):
                c, t = divmod(j, T)
                c0, r = chunk(u, c)
                if j == 0:
                    pe.wait_ge(*at(pe, "mrow_in", u, 16))
                    pe.wait_ge(*at(pe, "qexp_in", u, 16))
                    if u.L == 1:
                        pe.wait_ge(*at(pe, "maskexp_in", u, 32))
                pe.wait_ge(*at(pe, "probs_ready", u, j - SR + 1))
                ps = sexp[j % SR][0:r, 0:QW]
                last = pe.matmul(ps, krep[:, u.par, t, c0:c0 + r],
                                 qexp[:, u.par, t, :, :].rearrange("p h s -> p (h s)"), start=True, stop=not masks)
                if masks:
                    last = add_mask(ps, maskexp[:, u.par], 1, c, r)
                last.then_inc(sem["sexp_ready"], 1)

            def values(u, j):
                c, t = divmod(j, T)
                r = chunk(u, c)[1]
                if j == 0:
                    pe.wait_ge(*at(pe, "v_ready", u, G[u.L]))
                    pe.wait_ge(*at(pe, "acc_copied", u, 0))
                pe.wait_ge(*at(pe, "probs_ready", u, j + 1))
                for p in range(2):
                    q, slot = 2 * (t % 2) + p, t // 2
                    last = pe.matmul(acc[32 * q:32 * q + VW, 2 * S * slot:2 * S * slot + 2 * S],
                                     vx[0:r, u.par, PAIRS * c + 2 * t + p, :],
                                     probs[0:r, j % PR, 2 * S * p:2 * S * p + 2 * S],
                                     start=(c == 0 and slot == 0), stop=(c == CHUNKS[u.L][-1]), skip_group_check=True)
                last.then_inc(sem["pv_done"], 1)

            def output(u):
                pe.wait_ge(*at(pe, "acc_copied", u, 1))
                ps = begin("O", u)
                for t in range(T):
                    last = pe.transpose(ps[0:S, 128 * t:128 * t + 128], osb[:, S * t:S * t + S], ident[:, :])
                last.then_inc(sem["o_filled"], 1)

            def output_back(u):
                pe.wait_ge(*at(pe, "o_normal" if u.L else "o_read", u, 1))
                ps = begin("OT", u)
                pe.transpose(ps[:, 0:S], oatt[:, :], ident[0:S, 0:S]).then_inc(sem["oT_filled"], 1)

            def project(u):
                pe.wait_ge(*at(pe, "oT_ready", u, 1))
                ps = begin("wo", u)
                pe.matmul(ps[0:S, 0:D], oT[:, :], wo[:, u.L, :], start=True, stop=True).then_inc(sem["wo_filled"], 1)

            def feed_forward(u):
                pe.wait_ge(*at(pe, "oT_ready", u, 1))
                ps = begin("h", u)
                for j in range(FF // 128):
                    last = pe.matmul(ps[:, S * j:S * j + S], w1[:, 128 * j:128 * j + 128], oT[:, :], start=True, stop=True)
                last.then_inc(sem["h_filled"], 1)
                ps = begin("wo", u)
                for j in range(FF // 128):
                    last = pe.matmul(ps[0:S, 0:D], hT[:, j, :], w2[:, j, :], start=(j == 0), stop=(j == 3))
                last.then_inc(sem["wo_filled"], 1)

            def flag_sum():
                pe.wait_ge(sem["mask_counted"], 1)
                ps = begin("flag", None)
                pe.matmul(ps[0:1, 0:1], maskcount[:, :], ones[:, :], start=True, stop=True
                          ).then_inc(sem["flag_filled"], 1)

            def stage(s, n, masks=False, all_units=True):
                for j in range(NSTEP):
                    if s.exp is not None:
                        exp_scores(s.exp, j, masks and s.exp.L == 1)
                    for i in range(NPAIR):
                        if MAX_AT[i] == j and s.top is not None:
                            max_scores(s.top, i, masks and s.top.L == 1)
                    if s.post is not None and j < PVLAG:
                        values(s.post, NSTEP - PVLAG + j)
                    for i in range(NSTEP):
                        if VALUES_AT[i] == j and s.exp is not None:
                            values(s.exp, i)
                    for g in range(3):
                        if s.prep is not None and j == AT[f"ct{g}"]:
                            context(s.prep, g)
                        if s.prep is not None and j == AT[f"k{g}"]:
                            keys(s.prep, g)
                        if s.prep is not None and s.prep.L == 1 and j == AT[f"mk{g}"]:
                            mask(s.prep, g)
                        if s.top is not None and j == AT[f"v{g}"]:
                            vals(s.top, g)
                    if s.post is not None and j == AT["O"]:
                        output(s.post)
                    if s.post is not None and s.post.L < 3 and j == AT["OT"]:
                        output_back(s.post)
                    if s.post is not None and s.post.L < 3 and j == AT["wo"]:
                        project(s.post)
                    if s.prep is not None and j == AT["xT"]:
                        inputs(s.prep)
                    if s.prep is not None and j == AT["q"]:
                        queries(s.prep)
                    if s.top is not None and j == MT_AT:
                        maxima(s.top)
                    if s.top is not None and j == AT["mn"]:
                        maximum_rows(s.top)
                    if all_units and n == FLAG_STAGE and j == NSTEP - 1:
                        flag_sum()

            pe.wait_ge(sem["pool_ready"], 5)
            pe.wait_ge(sem["const_ready"], 1)
            pe.wait_ge(sem["vector_ready"], 1)
            pipeline(pe, ALL, stage, last=MASK_STAGE - 1)
            flag = pe.value_load(maskflag[0:1, 0:1])
            before = held[0]
            with pe.If(flag != 0):
                pipeline(pe, ALL, lambda s, n: stage(s, n, masks=True), first=MASK_STAGE)
            held[0] = before
            with pe.Else():
                pipeline(pe, ALL, stage, first=MASK_STAGE)
            with pe.Fori(1, B + 1) as b:
                u = Unit(2, -1, b, 0)
                held[0] = ("wo", Unit(2, -2, b, 0))
                pe.wait_ge(*at(pe, "x_next", Unit(1, B - 1), 1))
                context(u, 0)
                keys(u, 0)
                vals(u, 0)
                inputs(u)
                queries(u)
                for i in range(2):
                    max_scores(u, i, False)
                maxima(u)
                maximum_rows(u)
                for j in range(T):
                    exp_scores(u, j, False)
                    if j:
                        values(u, j - 1)
                values(u, T - 1)
                output(u)
                output_back(u)
                feed_forward(u)
            held[0] = ("wo", Unit(2, B - 1))
            pipeline(pe, LAST, lambda s, n: stage(s, n, all_units=False))

        @block.scalar
        def _(act):
            def context(u, g):
                _, c0, n, _ = groups(u)[g]
                act.wait_ge(*at(act, "ct_filled", u, g + 1))
                if g == 0:
                    act.wait_ge(*at(act, "ct_lo", u, 0))
                for dst, done in ((ctf[:, c0:c0 + n], False), (ct[:, u.par, 0, c0:c0 + n], True)):
                    if u.L:
                        op = act.copy(dst, shared[:, 0:n])
                    else:
                        op = act.mul(dst, shared[:, 0:n], cols[:, COLC["gkv"]:COLC["gkv"] + 1])
                op.then_inc(sem["ct_read"], 1)

            def keys(u, g):
                _, c0, n, _ = groups(u)[g]
                if g == 0:
                    for i in range(3):
                        act.wait_ge(*at(act, f"krep_in{i}", u, 0))
                act.wait_ge(*at(act, "k_filled", u, g + 1))
                for dst in (kf[:, c0:c0 + n], kp[:, 0, c0:c0 + n]):
                    if u.L:
                        bk = COLC[f"bk{u.L}"]
                        op = act.activation(dst, shared[:, 0:n], ACT.Identity, bias=cols[:, bk:bk + 1])
                    else:
                        op = act.copy(dst, shared[:, 0:n])
                op.then_inc(sem["k_read"], 1)

            def vals(u, g):
                chunks, _, _, r = groups(u)[g]
                act.wait_ge(*at(act, "v_filled", u, g + 1))
                a0, a1 = PAIRS * chunks[0], PAIRS * (chunks[-1] + 1)
                act.copy(vx[0:r, u.par, a0:a1, 0:2 * (DH + 1)].rearrange("p a (f e) -> p a f e", f=2)[:, :, :, 0:DH],
                         shared[0:r, 0:2 * DH * (a1 - a0)].rearrange("p (a f d) -> p a f d", f=2, d=DH)
                         ).then_inc(sem["v_ready"], 1)

            def mask_bytes(u):
                act.wait_ge(*at(act, "mask_loaded", u, 16))
                act.copy(maskb[:, :], mask8[:, :]).then_inc(sem["mask_copied"], 1)

            def mask(u, g):
                c0, r = GROUPS[g][0], ROWS[GROUPS[g][0]]
                act.wait_ge(*at(act, "mk_filled", u, g + 1))
                act.copy(maskmax[0:r, u.par, c0:c0 + 4, :], shared[0:r, :].bitcast(BF16)[:, 0:4 * S].rearrange(
                    "p (c s) -> p c s", c=4)).then_inc(sem["mask_ready"], 1)

            def input_copy(u):
                if u.L:
                    act.wait_ge(*at(act, "x_next", Unit(u.L - 1, u.batch, u.reg, 0), 1))
                act.copy(xcur[:, :], u.rows_of(xall)
                         ).then_inc(sem["x_copied"], 1)

            def inputs(u):
                act.wait_ge(*at(act, "xT_filled", u, 1))
                act.copy(xT[:, 0, :], shared[:, 0:S]).then_inc(sem["x_hi"], 1)

            def maximum_rows(u):
                act.wait_ge(*at(act, "mn_filled", u, 1))
                act.wait_ge(*at(act, "mrow_in", u, 0))
                act.copy(mrow[:, :], shared[0:H, :].bitcast(F16)[:, 0:S]).then_inc(sem["mrow_ready"], 1)

            def exps(u, j):
                r = chunk(u, j // T)[1]
                act.wait_ge(*at(act, "pv_done", u, j - PR + 1 if u.L != 2 else 0))
                if u.L == 2:
                    act.wait_ge(*at(act, "masked_ready", u, j + 1))
                    src = masked[:, j % 2, :]
                else:
                    act.wait_ge(*at(act, "sexp_ready", u, j + 1))
                    src = sexp[j % SR][0:r, 0:QW]
                act.activation(probs[0:r, j % PR, :], src, ACT.Exp).then_inc(sem["probs_ready"], 1)

            def accumulated(u):
                act.wait_ge(*at(act, "pv_done", u, STEPS[u.L]))
                act.copy(osb[:, :], acc[:, 0:QW]).then_inc(sem["acc_copied"], 1)

            def output_back(u):
                act.wait_ge(*at(act, "oT_filled", u, 1))
                act.copy(oT[:, :], shared[:, 0:S]).then_inc(sem["oT_ready"], 1)

            def stage(s, n, all_units=True):
                for j in range(NSTEP):
                    if s.exp is not None:
                        exps(s.exp, j)
                    if s.post is not None and j == ACC_AT:
                        accumulated(s.post)
                    for g in range(3):
                        if s.prep is not None and j == AT[f"ct{g}"]:
                            context(s.prep, g)
                        if s.prep is not None and j == AT[f"k{g}"]:
                            keys(s.prep, g)
                        if s.prep is not None and s.prep.L == 1 and j == AT[f"mk{g}"]:
                            mask(s.prep, g)
                        if s.top is not None and j == AT[f"v{g}"]:
                            vals(s.top, g)
                    if s.post is not None and s.post.L < 3 and j == AT["OT"]:
                        output_back(s.post)
                    if s.prep is not None and j == AT["xT"] - 1:
                        input_copy(s.prep)
                    if s.prep is not None and j == AT["xT"]:
                        inputs(s.prep)
                    if s.prep is not None and s.prep.L == 1 and j == AT["mk0"] - 1:
                        mask_bytes(s.prep)
                    if all_units and n == FLAG_STAGE - 1 and j == AT["v2"] + 1:
                        act.wait_ge(sem["mask_in_all"], 16)
                        act.activation(anymask[:, :], anymask[:, :], ACT.Copy, accum_out=maskcount[:, :]
                                       ).then_inc(sem["mask_counted"], 1)
                    if s.top is not None and j == AT["mn"]:
                        maximum_rows(s.top)
                    if all_units and n == FLAG_STAGE and j == NSTEP - 1:
                        act.wait_ge(sem["flag_filled"], 1)
                        act.copy(maskflag[:, :], shared[0:1, 0:1]).then_inc(sem["flag_ready"], 1)

            act.wait_ge(sem["pool_ready"], 5)
            act.wait_ge(sem["const_ready"], 1)
            act.wait_ge(sem["vector_ready"], 1)
            pipeline(act, ALL, stage)
            with act.Fori(1, B + 1) as b:
                u = Unit(2, -1, b, 0)
                context(u, 0)
                keys(u, 0)
                vals(u, 0)
                input_copy(u)
                inputs(u)
                maximum_rows(u)
                for j in range(T):
                    exps(u, j)
                accumulated(u)
                output_back(u)
                act.wait_ge(*at(act, "h_filled", u, 1))
                for j in range(FF // 128):
                    k = COLC["ffb0"] + j
                    act.activation(hT[:, j, :], shared[:, S * j:S * j + S], ACT.Gelu, bias=cols[:, k:k + 1]
                                   ).then_inc(sem["h_ready"], 1)
            pipeline(act, LAST, lambda s, n: stage(s, n, all_units=False))

        @block.vector
        def _(dve):
            counted = {}

            def own(name, u, op):
                counted[name] = counted.get(name, 0) + 1
                assert counted[name] <= PER[name][u.L]
                op.then_inc(sem[name], 1)
                dve.wait_ge(*at(dve, name, u, counted[name]))

            def power(u):
                dve.wait_ge(*at(dve, "ctx_loaded", u, 32))
                spans = ((0, 4, ROWS[0]), (4, NCH, ROWS[4]))
                for c0, c1, r in spans:
                    op = dve.tensor_tensor(sq[0:r, c0:c1, :], nat[0:r, c0:c1, :], nat[0:r, c0:c1, :], ALU.mult)
                own("own_power", u, op)
                for c0, c1, r in spans:
                    op = dve.tensor_reduce(ssq[0:r, c0:c1], sq[0:r, c0:c1, :], AX, ALU.add)
                own("own_power", u, op)
                for c0, c1, r in spans:
                    op = dve.tensor_scalar(ssq[0:r, c0:c1], ssq[0:r, c0:c1], 1.0 / D, EPS[0], ALU.mult, ALU.add)
                op.then_inc(sem["row_power"], 1)

            def inputs(u):
                dve.wait_ge(*at(dve, "x_hi", u, 1))
                dve.tensor_tensor(xT[:, 1, :], shared[:, 0:S], xT[:, 0, :], ALU.subtract).then_inc(sem["x_lo"], 1)

            def queries(u):
                dve.wait_ge(*at(dve, "q_filled", u, 1))
                dve.scalar_tensor_tensor(out=qf[:, :, :], in0=shared[0:PARTS, 0:T * S].rearrange("p (t s) -> p t s", t=T),
                                         scalar=SCALE, in1=bqs[:, u.L, :].unsqueeze(2).broadcast_to([PARTS, T, S]),
                                         op0=ALU.mult, op1=ALU.add).then_inc(sem["q_read"], 1)
                dve.wait_ge(*at(dve, "q_read", u, 1))
                dve.wait_ge(*at(dve, "q_spread", u, 0))
                own("own_q", u, dve.tensor_copy(qs[:, :, :], qf[:, :, :]))
                dve.tensor_tensor(qs[32:64, :, :], qf[32:64, :, :], qs[32:64, :, :], ALU.subtract
                                  ).then_inc(sem["q_parts"], 1)

            def maximum(u, i):
                c, t = divmod(2 * i, T)
                r = chunk(u, c)[1]
                dve.wait_ge(*at(dve, "smax_ready", u, i + 1))
                src = smax[i % SR][0:r, :].rearrange("p (k n) -> p k n", k=2)[:, :, 0:QW]
                dst = mx[0:r, QW * t:QW * t + 2 * QW].rearrange("p (k n) -> p k n", k=2)
                if u.L == 2:
                    for k in range(2):
                        v = "p (h s) -> p h s"
                        op = dve.tensor_tensor(dst[:, k, :].rearrange(v, h=HT), src[:, k, :].rearrange(v, h=HT),
                                               causal[:, 0, :].unsqueeze(1).broadcast_to([S, HT, S]), ALU.add)
                elif c == 0:
                    op = dve.tensor_copy(dst, src)
                else:
                    op = dve.tensor_tensor(dst, src, dst, ALU.max)
                op.then_inc(sem["smax_used"], 1)

            def maxima(u):
                n = chunk(u, 0)[1]
                for i in range(2):
                    dve.wait_ge(*at(dve, "mt_filled", u, i + 1))
                    dve.tensor_reduce(mneg[:, 8 * i:8 * i + 8],
                                      smax[0][0:S, 512 * i:512 * i + 512].bitcast(F16).rearrange(
                                          "s (h n) -> s h n", h=8)[:, :, 0:n], AX, ALU.max, negate=True
                                      ).then_inc(sem["m_ready"], 1)

            def causal_mask(u, j):
                dve.wait_ge(*at(dve, "sexp_ready", u, j + 1))
                dve.wait_ge(*at(dve, "probs_ready", u, j - 1))
                v = "p (h s) -> p h s"
                dve.tensor_tensor(masked[:, j % 2, :].rearrange(v, h=HT), sexp[j % SR][0:S, 0:QW].rearrange(v, h=HT),
                                  causal[:, 1, :].unsqueeze(1).broadcast_to([S, HT, S]), ALU.add
                                  ).then_inc(sem["masked_ready"], 1)

            def centre(u, src):
                own("own_ln", u, dve.tensor_reduce(mv[:, 0:1], src, AX, ALU.add))
                own("own_ln", u, dve.scalar_tensor_tensor(out=xn[:, :], in0=mv[:, 0:1].broadcast_to([S, D]),
                                                          scalar=-1.0 / D, in1=src, op0=ALU.mult, op1=ALU.add))
                own("own_ln", u, dve.tensor_tensor_reduce(squared[:, :], xn[:, :], xn[:, :], 1.0, 0.0, ALU.mult, ALU.add,
                                                          mv[:, 1:2]))
                dve.tensor_scalar(vare[:, :], mv[:, 1:2], 1.0 / D, EPS[u.L], ALU.mult, ALU.add
                                  ).then_inc(sem["var_ready"], 1)

            def scale(u, dst, done):
                dve.wait_ge(*at(dve, "rstd_ready", u, 1))
                own("own_ln", u, dve.scalar_tensor_tensor(out=xn[:, :], in0=xn[:, :], scalar=rstd[:, :],
                                                          in1=rows[:, ROW[f"g{u.L}"], :], op0=ALU.mult, op1=ALU.mult))
                dve.tensor_tensor(dst, xn[:, :], rows[:, ROW[f"b{u.L}"], :], ALU.add).then_inc(sem[done], 1)

            def residual(u):
                return u.rows_of(xall)

            def output(u):
                dve.wait_ge(*at(dve, "o_filled", u, 1))
                o = shared[0:S, :].rearrange("s (a f q v) -> s f a q v", a=2, f=2, q=4)
                sums = osum[:, :].rearrange("s (a q f) -> s f a q", a=2, q=4)
                to = oatt[:, :].rearrange("s (a q f d) -> s f a q d", a=2, q=4, f=2)
                for f in range(2):
                    op = dve.reciprocal(sums[:, f], o[:, f, :, :, (DH + 1) * f + DH])
                own("own_o", u, op)
                for f in range(2):
                    op = dve.tensor_tensor(to[:, f], o[:, f, :, :, (DH + 1) * f:(DH + 1) * f + DH],
                                           sums[:, f].unsqueeze(3).broadcast_to([S, 2, 4, DH]), ALU.mult)
                op.then_inc(sem["o_read"], 1)
                if u.L == 0:
                    return
                dve.wait_ge(*at(dve, "o_read", u, 1))
                bv = rows[:, ROW[f"bv{u.L}"], :]
                if u.L == 1:
                    dve.tensor_tensor(oatt[:, :], oatt[:, :], bv, ALU.add).then_inc(sem["o_normal"], 1)
                    return
                name = "own_o" if u.L == 3 else "own_y"
                own(name, u, dve.tensor_tensor(y[:, :], oatt[:, :], bv, ALU.add))
                own(name, u, dve.tensor_tensor(y[:, :], y[:, :], residual(u), ALU.add))
                centre(u, y[:, :])

            def projected(u):
                dve.wait_ge(*at(dve, "wo_filled", u, 1))
                dve.tensor_tensor(y[:, :], shared[0:S, 0:D], rows[:, ROW[f"bo{u.L}"], :], ALU.add
                                  ).then_inc(sem["wo_read"], 1)
                dve.wait_ge(*at(dve, "wo_read", u, 1))
                if u.L == 0:
                    dve.tensor_tensor(residual(u), y[:, :], residual(u), ALU.add).then_inc(sem["x_next"], 1)
                    return
                own("own_y", u, dve.tensor_tensor(y[:, :], y[:, :], residual(u), ALU.add))
                centre(u, y[:, :])

            def stage(s, n):
                counted.clear()
                for j in range(NSTEP):
                    for i in range(NPAIR):
                        if MAX_AT[i] == j and s.top is not None:
                            maximum(s.top, i)
                    if s.post is not None and j == AT["O"] + 1:
                        output(s.post)
                    if s.post is not None and s.post.L < 3 and j == AT["wo"] + 1:
                        projected(s.post)
                    if s.prep is not None and j == AT["xT"]:
                        inputs(s.prep)
                    if s.prep is not None and j == AT["q"]:
                        queries(s.prep)
                    if s.post is not None and s.post.L == 1 and j == AT["q"] + 3:
                        scale(s.post, residual(s.post), "x_next")
                    if s.post is not None and s.post.L == 3 and j == AT["q"] + 3:
                        dve.wait_ge(*at(dve, "out_sent", s.post, 0))
                        scale(s.post, outsb[:, :], "out_ready")
                    if s.load is not None and s.load.L == 0 and j == AT["v2"] + 3:
                        power(s.load)
                    if s.top is not None and j == MT_AT:
                        maxima(s.top)

            steps = [0]

            def step(op):
                steps[0] += 1
                op.then_inc(sem["setup"], 1)
                dve.wait_ge(sem["setup"], steps[0])

            dve.wait_ge(sem["const_in"], 16 * 13)
            dve.memset(krep[PARTS:PARTS + 1, :, :, :], 1.0).then_inc(sem["const_ready"], 1)
            dve.tensor_copy(ident16[:, :], ident[:, :])
            dve.tensor_copy(identb[:, :], ident[:, :])
            for i in range(2):
                dve.tensor_scalar(masked_by[:, i, :], ident[:, :], MASKED[i], None, ALU.mult)
            dve.memset(ones[:, :], 1.0)
            dve.tensor_copy(headmask16[:, :], headmask[:, :])
            dve.tensor_scalar(bqs[:, :, :], bq[:, :, :], SCALE, None, ALU.mult)
            for w, high, low in ((wq[:, :, :, :], wq16[:, 0], wq16[:, 1]), (wk[:, :, :], wk16[:, 0], wk16[:, 1]),
                                 (wv[:, :, :], wv16[:, 0], wv16[:, 1])):
                step(dve.tensor_copy(high, w))
                dve.tensor_tensor(low, w, high, ALU.subtract)
            step(dve.tensor_tensor(sq[0:S, 0:B, :], xall[:, :, :], xall[:, :, :], ALU.mult))
            step(dve.tensor_reduce(ssq[0:S, 0:B], sq[0:S, 0:B, :], AX, ALU.add))
            dve.tensor_scalar(ssq[0:S, 0:B], ssq[0:S, 0:B], 1.0 / D, EPS[0], ALU.mult, ALU.add
                              ).then_inc(sem["x_power"], 1)
            dve.wait_ge(sem["x_root"], 1)
            step(dve.tensor_tensor(xall[:, :, :], xall[:, :, :],
                                   rinv[0:S, 0:B].unsqueeze(2).broadcast_to([S, B, D]), ALU.mult))
            dve.tensor_tensor(xall[:, :, :], xall[:, :, :],
                              rows[:, ROW["gq"], :].unsqueeze(1).broadcast_to([S, B, D]), ALU.mult
                              ).then_inc(sem["vector_ready"], 1)
            dve.wait_ge(sem["vector_ready"], 1)
            pipeline(dve, ALL, stage)
            with dve.Fori(1, B + 1) as b:
                u = Unit(2, -1, b, 0)
                counted.clear()
                inputs(u)
                queries(u)
                for i in range(2):
                    maximum(u, i)
                maxima(u)
                for j in range(T):
                    causal_mask(u, j)
                output(u)
                scale(u, oatt[:, :], "o_normal")
                dve.wait_ge(*at(dve, "o_normal", u, 1))
                dve.wait_ge(*at(dve, "wo_filled", u, 1))
                dve.tensor_tensor(y[:, :], shared[0:S, 0:D], rows[:, ROW["ff2"], :], ALU.add
                                  ).then_inc(sem["wo_read"], 1)
                dve.wait_ge(*at(dve, "wo_read", u, 1))
                dve.tensor_tensor(residual(u), y[:, :], oatt[:, :], ALU.add).then_inc(sem["x_next"], 1)
            pipeline(dve, LAST, stage)


def kernel(**inputs):
    import concourse.bacc as _bacc
    from concourse.bass_utils import run_bass_kernel_spmd as _run

    a = {k: np.asarray(v) for k, v in inputs.items()}
    wq = np.stack([a["L0_xattn_wq"].T, a["L1_xattn_Wq"].T, a["L2_xattn_Wq"].T, a["L3_xattn_Wq"]])
    wk = np.stack([a["L0_xattn_wk"].T, a["L1_xattn_Wk"].T, a["L2_xattn_Wk"].T, a["L3_xattn_Wk"]])
    wv = np.stack([a["L0_xattn_wv"].T, a["L1_xattn_Wv"].T, a["L2_xattn_Wv"].T, a["L3_xattn_Wv"]])
    wq3 = np.concatenate([wq.reshape(4, D, T, 1, 32)] * 3, axis=3).reshape(4, D, T * PARTS)
    row = {"gq": "L0_xattn_gq", "bo0": "L0_xattn_bo", "bv1": "L1_xattn_bv", "bo1": "L1_xattn_bo",
           "g1": "L1_xattn_gamma", "b1": "L1_xattn_beta", "bv2": "L2_xattn_bv", "g2": "L2_xattn_ln_g",
           "b2": "L2_xattn_ln_b", "ff2": "L2_xattn_b2", "bv3": "L3_xattn_bv", "g3": "L3_xattn_ln_gamma",
           "b3": "L3_xattn_ln_beta"}
    rows = np.stack([a[row[n]] for n in ROW])
    b1 = a["L2_xattn_b1"].reshape(FF // 128, 128)
    cols = np.stack([a["L0_xattn_gkv"], a["L1_xattn_bk"], a["L2_xattn_bk"], a["L3_xattn_bk"], *b1], axis=1)
    zero = np.zeros(D, np.float32)
    bq = np.stack([zero, a["L1_xattn_bq"], a["L2_xattn_bq"], a["L3_xattn_bq"]]).reshape(4, T, 1, 32)
    bq = np.concatenate([bq] * 3, axis=2).reshape(4, T, PARTS).transpose(2, 0, 1)
    headmask = np.zeros((PARTS, HT), np.float32)
    for p in range(PARTS):
        headmask[p, p % 32 // DH] = 1.0
    later = np.arange(S)[:, None] > np.arange(S)[None, :]
    causal = np.zeros((S, 2, S), np.float32)
    causal[:, 0][later] = -30000.0
    causal[:, 1][later] = -1e9
    arrays = {
        "ctx": a["ctx_1024"], "x": a["x"], "mask": a["mask_Bx1xSxS2_bf0"], "w_qkv": np.concatenate([wq3, wk, wv], axis=2),
        "w_o": np.stack([a["L0_xattn_wo"].T, a["L1_xattn_Wo"].T]), "w_1": a["L2_xattn_W1"].T, "w_2": a["L2_xattn_W2"].T,
        "rows": np.broadcast_to(rows, (S,) + rows.shape), "cols": cols, "bq": bq, "headmask": headmask,
        "ident": np.eye(128, dtype=np.float32)[None], "causal": causal,
    }
    nc = _bacc.Bacc("TRN2", target_bir_lowering=False, num_devices=1)
    args = []
    for name, value in arrays.items():
        arrays[name] = np.ascontiguousarray(value)
        args.append(nc.dram_tensor(f"in_{name}", value.shape, U8 if name == "mask" else F32, kind="ExternalInput").ap())
    out = nc.dram_tensor("out_0", (B, S, D), F32, kind="ExternalOutput").ap()
    build(nc, *args, out)
    r = _run(nc, [{f"in_{k}": v for k, v in arrays.items()}], core_ids=[0])
    return r.results[0]["out_0"]
```

```python
from contextlib import ExitStack

import numpy as np

import concourse.bass as bass
from concourse import mybir

F32 = mybir.dt.float32
F16 = mybir.dt.float16
BF16 = mybir.dt.bfloat16
U8 = mybir.dt.uint8
I32 = mybir.dt.int32
ALU = mybir.AluOpType
ACT = mybir.ActivationFunctionType
AX = mybir.AxisListType.X

B, S, D = 8, 100, 128
KEYS = 1444
H, DH = 16, 8
T, HT = 4, 4
QW = HT * S
FF = 512
NCH = 12
LONG = KEYS - (KEYS // NCH) * NCH
ROWS = [KEYS // NCH + (c < LONG) for c in range(NCH)]
COL = [sum(ROWS[:c]) for c in range(NCH + 1)]
SPANS = [(0, 4, ROWS[0]), (4, NCH, ROWS[4])]
GROUPS = [range(0, 4), range(4, 8), range(8, 12)]
SCALE = float(DH) ** -0.5
MASKED = [-30000.0, -1e30]
VW = 32
PAIRS = H // 2
PR, SR, MR = 6, 2, 3
PARTS = 3 * 32

TWO_ONES = float(np.ones(2, np.float16).view(np.float32)[0])

ROW = {n: i for i, n in enumerate(
    ["gq", "bo0", "bv1", "bo1", "g1", "b1", "bv2", "g2", "b2", "ff2", "bv3", "g3", "b3"])}
COLC = {n: i for i, n in enumerate(["gkv", "bk1", "bk2", "bk3", "bq2", "ffb0", "ffb1", "ffb2", "ffb3"])}

NG = [3, 3, 0, 3]
STEPS = [T * NCH, T * NCH, 0, T * NCH]
EPS = [1e-6, 1e-5, 1e-5, 1e-6]

NSTEP = NCH * T
AT = {"ct0": 0, "ct1": 3, "ct2": 6, "O": 7, "k0": 9, "OT": 11, "k1": 12, "wo": 14, "k2": 15, "xT": 17, "q": 19,
      "v0": 22, "v1": 24, "v2": 26, "mk0": 28, "mk1": 30, "mk2": 32, "mn": 42}
AT2 = {"cx": 4, "kqv": 10, "s0": 16, "s1": 18, "s2": 20, "s3": 21, "max": 22, "exp": 28, "pt0": 30, "pt1": 32,
       "pt2": 34, "pt3": 36, "o": 40, "scale": 45}
AT2_FF = {"at": 1, "h": 8, "w2": 13}
BANK = {"ct0": 0, "ct1": 1, "ct2": 0, "O": 1, "k0": 0, "OT": 1, "k1": 0, "wo": 1, "k2": 0, "xT": 1, "q": 0, "v0": 1,
        "v1": 0, "v2": 1, "mk0": 0, "mk1": 1, "mk2": 0, "mn": 1, "flag": 1}
BANK3 = {"ct0": 0, "at2": 1, "ct1": 0, "cx2": 1, "ct2": 0, "O": 1, "h2": 0, "k0": 1, "kqv2": 0, "k1": 1, "w2": 0, "k2": 1,
         "s20": 0, "xT": 1, "s21": 0, "q": 1, "s22": 0, "s23": 1, "v0": 0, "v1": 1, "v2": 0, "pt20": 1, "pt21": 0,
         "pt22": 1, "pt23": 0, "o2": 1, "mn": 0}
PVLAG = 3
VALUES_AT = [5, 5, 6, 6] + [j + PVLAG for j in range(4, NSTEP)]
MAX_AT = [i * 39 // NSTEP for i in range(NSTEP)]
MT_AT = 39
ACC_AT = 3


class Unit:
    def __init__(self, layer, batch, reg=None, parity=None):
        self.L, self.batch, self.reg = layer, batch, reg
        self.par = batch % 2 if parity is None else parity

    def rows_of(self, tile):
        if self.reg is None:
            return tile[:, self.batch, :]
        return tile[:, bass.ds(self.reg + self.batch if self.batch else self.reg, 1), :].rearrange("s a d -> s (a d)")


def build(nc, ctx_in, x_in, mask_in, w_qkv, w_o, w_1, w_2, rows_in, cols_in, bq_in, headmask_in, heads_in, ident_in,
          causal_in, out):
    with ExitStack() as es:
        def sb(name, shape, dt=F32):
            return es.enter_context(nc.sbuf_tensor(name, shape, dt))

        def psum(name, banks=1):
            return es.enter_context(nc.psum_tensor(name, [128, 512 * banks], F32))

        wq = sb("wq", [128, 4, T, PARTS])
        wk = sb("wk", [128, 4, D])
        wv = sb("wv", [128, 4, D])
        wo = sb("wo", [128, 2, D])
        w1 = sb("w1", [128, FF])
        w2 = sb("w2", [128, FF // 128, D])
        wq16 = sb("wq16", [128, 2, 4, T, PARTS], F16)
        wk16 = sb("wk16", [128, 2, 4, D], F16)
        wv16 = sb("wv16", [128, 2, 4, D], F16)
        rows = sb("rows", [S, len(ROW), D])
        cols = sb("cols", [128, len(COLC)])
        bq = sb("bq", [PARTS, 4, T])
        bqs = sb("bqs", [PARTS, 4, T])
        headmask = sb("headmask", [PARTS, HT])
        headmask16 = sb("headmask16", [PARTS, HT], F16)
        ident = sb("ident", [128, 128])
        ident16 = sb("ident16", [128, 128], F16)
        identb = sb("identb", [128, 128], BF16)
        masked_by = sb("masked_by", [128, 2, 128], BF16)
        causal = sb("causal", [S, S])
        heads = sb("heads", [128, H])
        bq2 = sb("bq2", [128, 1])
        half = sb("half", [128, NCH])
        ones = sb("ones", [128, 1])
        anymask = sb("anymask", [128, B * S * KEYS // 128], U8)
        maskcount = sb("maskcount", [128, 1])
        maskflag = sb("maskflag", [1, 1], I32)
        xall = sb("xall", [S, B, D])
        ssqx = sb("ssqx", [S, B])
        rinvx = sb("rinvx", [S, B])
        mask8 = sb("mask8", [S, KEYS], U8)
        maskb = sb("maskb", [S, KEYS], BF16)
        maskmax = sb("maskmax", [128, 2, NCH, S], BF16)
        maskexp = sb("maskexp", [128, 2, NCH, S], BF16)
        nat = sb("nat", [128, NCH, D])
        sq = sb("sq", [128, NCH, D])
        ssq = sb("ssq", [128, NCH])
        rinv = sb("rinv", [128, NCH])
        ctf = sb("ctf", [128, KEYS])
        ct = sb("ct", [128, 2, 2, KEYS], F16)
        kf = sb("kf", [128, KEYS])
        kp = sb("kp", [128, 2, KEYS], F16)
        krep = sb("krep", [PARTS + 1, 2, T, KEYS], F16)
        vx = sb("vx", [128, 2, NCH * PAIRS, VW])
        xcur = sb("xcur", [S, D])
        xT = sb("xT", [128, 2, S], F16)
        qf = sb("qf", [PARTS, T, S])
        qs = sb("qs", [PARTS, T, S], F16)
        qmax = sb("qmax", [PARTS, 2, T, HT, S], F16)
        qexp = sb("qexp", [PARTS + 1, 2, T, HT, S], F16)
        mx = sb("mx", [128, T * QW], F16)
        mneg = sb("mneg", [S, H], F16)
        mrow = sb("mrow", [H, S], F16)
        probs = sb("probs", [128, PR, QW])
        osb = sb("osb", [128, QW])
        osum = sb("osum", [S, 2, H])
        oatt = sb("oatt", [S, 2, D])
        oT = sb("oT", [128, S])
        y = sb("y", [S, 2, D])
        squared = sb("squared", [S, 2, D])
        mv = sb("mv", [S, 2, 2])
        vare = sb("vare", [S, 2])
        rstd = sb("rstd", [S, 2])
        xn = sb("xn", [S, 2, D])
        nat2 = sb("nat2", [S, D])
        x2 = sb("x2", [S, D])
        cx2 = sb("cx2", [128, 2, S])
        k2 = sb("k2", [128, S])
        q2 = sb("q2", [128, S])
        v2 = sb("v2", [S, H, DH + 1])
        kbd2 = sb("kbd2", [128, H, S])
        sc2 = sb("sc2", [S, H, S])
        max2 = sb("max2", [S, H])
        pT2 = sb("pT2", [S, H, S])
        att2 = sb("att2", [S, D])
        aT2 = sb("aT2", [128, S])
        hT = sb("hT", [128, FF // 128, S])
        outsb = sb("outsb", [S, D])

        smax = [psum(f"smax{i}") for i in range(MR)]
        sexp = [psum(f"sexp{i}") for i in range(SR)]
        acc = psum("acc")
        shared = [psum(f"shared{i}") for i in range(2)]

        G = NG
        one, no2 = [1, 1, 0, 1], [1, 1, 0, 0]
        PER = {
            "ctx_loaded": [32, 32, 0, 32], "row_power": [1, 0, 0, 0], "ctx_normal": [1, 0, 0, 0],
            "ct_filled": G, "ct_read": G, "ct_lo": G, "k_filled": G, "k_read": G, "k_lo": G,
            "x_copied": one, "xT_filled": one, "x_hi": one, "x_lo": one, "q_filled": one, "q_read": one,
            "q_parts": one, "q_spread": one, "qexp_in": [16, 16, 0, 16], "v_filled": G, "v_ready": G,
            "mask_loaded": [0, 16, 0, 0], "mask_copied": [0, 1, 0, 0], "mk_filled": [0, 3, 0, 0],
            "mask_ready": [0, 3, 0, 0], "maskexp_in": [0, 32, 0, 0],
            "smax_ready": STEPS, "smax_used": STEPS, "mt_filled": [2, 2, 0, 2],
            "m_ready": [2, 2, 0, 2], "mn_filled": one, "mrow_ready": one, "mrow_in": [16, 16, 0, 16],
            "sexp_ready": STEPS, "probs_ready": STEPS, "pv_done": STEPS,
            "acc_copied": one, "o_filled": one, "o_read": one, "o_normal": [0, 1, 0, 0], "oT_filled": no2,
            "oT_ready": no2, "wo_filled": no2, "wo_read": no2,
            "var_ready": [0, 1, 0, 1], "rstd_ready": [0, 1, 0, 1], "x_next": no2, "out_ready": [0, 0, 0, 1],
            "out_sent": [0, 0, 0, 16],
            "own_power": [1, 0, 0, 0], "squares_ready": [1, 0, 0, 0], "own_q": one, "own_o": [1, 1, 0, 3], "own_y": [0, 1, 0, 0],
            "own_ln": [0, 4, 0, 4], "own_rinv": [1, 0, 0, 0],
        }
        for g in range(3):
            PER[f"krep_in{g}"] = [16 * 12 * bool(n) for n in NG]
        for name, per in {"nat2_in": 32, "cx2_filled": 1, "cx2_read": 1, "kqv2_filled": 1, "kqv2_read": 1,
                          "kbd2_ready": 1, "s2_filled": 4, "s2_read": 4, "max2_ready": 1, "less2_ready": 1,
                          "exp2_ready": 1, "pt2_filled": 4, "pt2_read": 4, "o2_filled": 1, "o2_read": 1,
                          "var2_ready": 1, "rstd2_ready": 1, "att2_ready": 1, "at2_filled": 1, "at2_read": 1,
                          "h2_filled": 1, "h2_read": 4, "w2_filled": 1, "w2_read": 1, "x2_next": 1, "own_2": 7}.items():
            PER[name] = [0, 0, per, 0]
        setup_names = ["const_in", "pool_ready", "ones_ready", "wk_ready", "x_ready", "rest_ready", "x_power", "x_root", "setup",
                       "mask_in_all", "mask_counted", "flag_filled", "flag_ready"]
        sem = {name: es.enter_context(nc.semaphore(name)) for name in list(PER) + setup_names}
        READ = {"xT": ("x_lo", 1), "q": ("q_read", 1), "mn": ("mrow_ready", 1), "O": ("o_read", 1),
                "OT": ("oT_ready", 1), "wo": ("wo_read", 1), "cx2": ("cx2_read", 1), "kqv2": ("kqv2_read", 1),
                "o2": ("o2_read", 1), "at2": ("at2_read", 1), "h2": ("h2_read", 4), "w2": ("w2_read", 1)}
        for t in range(T):
            READ[f"s2{t}"] = ("s2_read", t + 1)
            READ[f"pt2{t}"] = ("pt2_read", t + 1)
        for g in range(3):
            READ[f"ct{g}"] = ("ct_read", g + 1)
            READ[f"k{g}"] = ("k_read", g + 1)
            READ[f"v{g}"] = ("v_ready", g + 1)
            READ[f"mk{g}"] = ("mask_ready", g + 1)

        registers = {}

        def at(engine, name, u, k):
            per = PER[name][u.L]
            value = B * sum(PER[name][:u.L]) + per * u.batch + k
            if u.reg is None or not per:
                return sem[name], max(value, 0)
            if engine not in registers:
                registers[engine] = ([engine.alloc_register(f"count{i}") for i in range(4)], {})
            counts, products = registers[engine]
            if per > 1 and (per not in products or products[per][1] is not u.reg):
                product = products[per][0] if per in products else engine.alloc_register(f"times{per}")
                engine.reg_mul(product, u.reg, per)
                products[per] = (product, u.reg)
            term = products[per][0] if per > 1 else u.reg
            if value == 0:
                return sem[name], term
            counts.append(counts.pop(0))
            engine.reg_add(counts[-1], term, value)
            return sem[name], counts[-1]

        def groups():
            return [(list(g), COL[g[0]], COL[g[-1] + 1] - COL[g[0]], ROWS[g[0]]) for g in GROUPS]

        def chunk(c):
            return COL[c], ROWS[c]

        class Stage:
            def __init__(self, load=None, prep=None, top=None, exp=None, post=None):
                self.load, self.prep, self.top, self.exp, self.post = load, prep, top, exp, post
                self.att2, self.ff2 = [Unit(2, u.batch, u.reg, u.par) if u is not None and u.L == 3 else None
                                       for u in (load, prep)]

        def stage_of(n, units, reg=None, base=0):
            def unit(i):
                if not 0 <= i < len(units):
                    return None
                u = units[i]
                if reg is None:
                    return u
                return Unit(u.L, u.batch - units[base].batch, reg, u.par)
            return Stage(unit(n + 3), unit(n + 2), unit(n + 1), unit(n), unit(n - 1))

        def pipeline(engine, units, run, first=-3, last=None):
            n = first
            last = len(units) if last is None else last
            while n <= last:
                b0 = units[n].batch if 0 <= n < len(units) else None
                if b0 == 1 and n + 3 <= last:
                    for i in range(2):
                        await_read(engine, i)
                    with engine.Fori(1, 4, 2) as b:
                        enter_loop(n, units, b)
                        run(stage_of(n, units, b, n), n)
                        run(stage_of(n + 1, units, b, n), n)
                        leave_loop(n, units, b)
                    n += 4
                else:
                    run(stage_of(n, units), n)
                    n += 1

        def bank(use, u):
            return BANK3[use] if u is not None and u.L >= 2 else BANK[use]

        held = [None, None]

        def last_uses(s):
            ends = [(AT["v1"], "v1", s.top), (AT["mk2"], "mk2", s.prep if s.prep.L == 1 else None),
                    (AT["mn"], "mn", s.top), (AT2["o"], "o2", s.att2)]
            for _, use, u in sorted((x for x in ends if x[2] is not None), key=lambda x: x[0]):
                held[bank(use, u)] = (use, u)

        def await_read(pe, i):
            if held[i] is not None:
                use, u = held[i]
                if use == "flag":
                    pe.wait_ge(sem["flag_ready"], 1)
                else:
                    pe.wait_ge(*at(pe, READ[use][0], u, READ[use][1]))

        def enter_loop(n, units, b):
            if held != [None, None]:
                last_uses(stage_of(n - 1, units, b, n))

        def leave_loop(n, units, b):
            for i in range(2):
                if held[i] is not None and held[i][1].reg is not None:
                    use, u = held[i]
                    held[i] = (use, Unit(u.L, u.batch + units[n + 2].batch, None, u.par))

        UNITS = [Unit(layer, b) for layer in (0, 1, 3) for b in range(B)]
        FLAG_STAGE = 0
        MASK_STAGES = B - 1, 2 * B - 1

        block = es.enter_context(nc.Block())

        @block.sync
        def _(sp):
            def batch_of(array, u):
                size = int(np.prod(array.shape[1:]))
                flat = array.rearrange(" ".join("abcd"[:len(array.shape)]) + " -> (" + " ".join(
                    "abcd"[:len(array.shape)]) + ")")
                start = u.batch if u.reg is None else u.reg + u.batch
                return flat[bass.ds(start * size, size)]

            def wait_alone(count, u):
                if u.reg is not None:
                    sp.wait_ge(sem["const_in"], 16 * 14)
                sp.wait_ge(*count)

            def load(u):
                src = batch_of(ctx_in, u)
                count = at(sp, "ct_filled", u, 0)
                wait_alone(count, u)
                full = KEYS // NCH
                sp.dma_start(nat[0:full, :, :], src[0:full * NCH * D].rearrange("(p c d) -> p c d", c=NCH, d=D)
                             ).then_inc(sem["ctx_loaded"], 16)
                sp.dma_start(nat[full:full + 1, 0:LONG, :], src[full * NCH * D:KEYS * D].rearrange("(b c d) -> b c d", b=1, d=D)
                             ).then_inc(sem["ctx_loaded"], 16)

            def load2(u):
                src = batch_of(ctx_in, u)
                counts = at(sp, "x_next", Unit(1, u.batch, u.reg), 1), at(sp, "cx2_filled", u, 0)
                sp.wait_ge(*counts[0])
                wait_alone(counts[1], u)
                sp.dma_start(x2[:, :], u.rows_of(xall)).then_inc(sem["nat2_in"], 16)
                sp.dma_start(nat2[:, :], src[0:S * D].rearrange("(s d) -> s d", d=D)).then_inc(sem["nat2_in"], 16)

            def replicate(u, g, before, steps):
                _, c0, n, _ = groups()[g]
                counts = [at(sp, "k_lo", u, g + 1)]
                if before is not None:
                    counts.append(at(sp, "sexp_ready", before, steps))
                for count in counts:
                    sp.wait_ge(*count)
                for t in range(T):
                    for j, part in enumerate((0, 0, 1)):
                        sp.dma_start(krep[32 * j:32 * j + 32, u.par, t, c0:c0 + n],
                                     kp[32 * t:32 * t + 32, part, c0:c0 + n]).then_inc(sem[f"krep_in{g}"], 16)

            def exp_copies(u, before):
                counts = [at(sp, "q_spread", u, 1)]
                if before is not None:
                    counts.append(at(sp, "sexp_ready", before, 1))
                for count in counts:
                    sp.wait_ge(*count)
                sp.dma_start(qexp[0:PARTS, u.par, :, :, :].rearrange("p t h s -> p (t h s)"),
                             qmax[:, u.par, :, :, :].rearrange("p t h s -> p (t h s)")).then_inc(sem["qexp_in"], 16)
                if u.L == 1:
                    sp.wait_ge(*at(sp, "mask_ready", u, 3))
                    full = KEYS // NCH
                    sp.dma_start(maskexp[0:full, u.par, :, :], maskmax[0:full, u.par, :, :]
                                 ).then_inc(sem["maskexp_in"], 16)
                    sp.dma_start(maskexp[full:full + 1, u.par, 0:LONG, :], maskmax[full:full + 1, u.par, 0:LONG, :]
                                 ).then_inc(sem["maskexp_in"], 16)

            def maximum_row(u):
                sp.wait_ge(*at(sp, "mrow_ready", u, 1))
                sp.dma_start(qexp[PARTS:PARTS + 1, u.par, :, :, :].rearrange("o t h s -> o (t h) s"), mrow[:, :]
                             ).then_inc(sem["mrow_in"], 16)

            def store(u):
                dst = batch_of(out, u)
                count = at(sp, "out_ready", u, 1)
                wait_alone(count, u)
                sp.dma_start(dst.rearrange("(s d) -> s d", d=D), outsb[:, :]
                             ).then_inc(sem["out_sent"], 16)

            def stage(s, n):
                if s.att2 is not None:
                    load2(s.att2)
                if s.top is not None:
                    replicate(s.top, 2, s.post, NSTEP)
                    exp_copies(s.top, s.exp)
                if s.prep is not None and s.prep.L == 1:
                    src = batch_of(mask_in, s.prep)
                    count = at(sp, "mask_copied", s.prep, 0)
                    wait_alone(count, s.prep)
                    sp.dma_start(mask8[:, :], src.rearrange("(s k) -> s k", k=KEYS)
                                 ).then_inc(sem["mask_loaded"], 16)
                if s.load is not None:
                    load(s.load)
                if s.prep is not None:
                    replicate(s.prep, 0, s.exp, NSTEP // 3)
                if s.post is not None and s.post.L == 3:
                    store(s.post)
                if s.prep is not None:
                    replicate(s.prep, 1, s.exp, 2 * NSTEP // 3)
                if s.top is not None:
                    maximum_row(s.top)

            def load_constants():
                for dst, src in ((ident[:, :], ident_in[0]), (xall[:, :, :], x_in.rearrange("b s d -> s b d")),
                                 (rows[:, :, :], rows_in), (cols[:, :], cols_in),
                                 (wk[:, :, :], w_qkv[:, :, T * PARTS:T * PARTS + D].rearrange("l c n -> c l n")),
                                 (wq[:, :, :, :], w_qkv[:, :, 0:T * PARTS].rearrange("l c (t p) -> c l t p", t=T)),
                                 (wv[:, :, :], w_qkv[:, :, T * PARTS + D:T * PARTS + 2 * D].rearrange("l c n -> c l n")),
                                 (wo[:, :, :], w_o.rearrange("l c n -> c l n")), (w1[:, :], w_1),
                                 (w2[:, :, :], w_2.rearrange("(j f) n -> f j n", f=128)),
                                 (bq[:, :, :], bq_in), (headmask[:, :], headmask_in), (heads[:, :], heads_in),
                                 (causal[:, :], causal_in)):
                    sp.dma_start(dst, src).then_inc(sem["const_in"], 16)

            def run(s, n):
                stage(s, n)
                if n == -3:
                    load_constants()
                    sp.dma_start(anymask[:, :], mask_in.rearrange("b o s k -> (b o s k)").rearrange(
                        "(p n) -> p n", p=128)).then_inc(sem["mask_in_all"], 16)

            pipeline(sp, UNITS, run)
            sp.wait_ge(sem["out_sent"], 16 * B)

        @block.gpsimd
        def _(pool):
            def low_part(u, g, src, dst, reads, done):
                _, c0, n, _ = groups()[g]
                pool.wait_ge(*at(pool, reads, u, g + 1))
                pool.tensor_tensor(dst[:, 1, c0:c0 + n], src[:, c0:c0 + n], dst[:, 0, c0:c0 + n], ALU.subtract
                                   ).then_inc(sem[done], 1)

            def root(u):
                k, names = (1, ("var2_ready", "rstd2_ready")) if u.L == 2 else (0, ("var_ready", "rstd_ready"))
                pool.wait_ge(*at(pool, names[0], u, 1))
                pool.tensor_tensor(rstd[:, k:k + 1], vare[:, k:k + 1], half[0:S, 0:1], ALU.pow).then_inc(sem[names[1]], 1)

            def spread2(u):
                pool.wait_ge(*at(pool, "kqv2_read", u, 1))
                pool.tensor_tensor(kbd2[:, :, :], k2[:, :].unsqueeze(1).broadcast_to([128, H, S]),
                                   heads[:, :].unsqueeze(2).broadcast_to([128, H, S]), ALU.mult
                                   ).then_inc(sem["kbd2_ready"], 1)

            def less_maximum(u):
                pool.wait_ge(*at(pool, "max2_ready", u, 1))
                pool.tensor_tensor(sc2[:, :, :], sc2[:, :, :], max2[:, :].unsqueeze(2).broadcast_to([S, H, S]), ALU.add
                                   ).then_inc(sem["less2_ready"], 1)

            def spread(u, before):
                if before is not None:
                    pool.wait_ge(*at(pool, "smax_used", before, 0))
                    pool.wait_ge(*at(pool, "qexp_in", before, 0))
                pool.wait_ge(*at(pool, "q_parts", u, 1))
                for t in range(T):
                    last = pool.tensor_tensor(qmax[:, u.par, t, :, :],
                                              qs[:, t, :].unsqueeze(1).broadcast_to([PARTS, HT, S]),
                                              headmask16[:, :].unsqueeze(2).broadcast_to([PARTS, HT, S]), ALU.mult)
                last.then_inc(sem["q_spread"], 1)

            def squares(u):
                pool.wait_ge(*at(pool, "ctx_loaded", u, 32))
                for c0, c1, r in SPANS:
                    last = pool.tensor_tensor(sq[0:r, c0:c1, :], nat[0:r, c0:c1, :], nat[0:r, c0:c1, :], ALU.mult)
                last.then_inc(sem["squares_ready"], 1)

            def normalise(u):
                pool.wait_ge(*at(pool, "row_power", u, 1))
                for c0, c1, r in SPANS:
                    last = pool.tensor_tensor(rinv[0:r, c0:c1], ssq[0:r, c0:c1], half[0:r, c0:c1], ALU.pow)
                last.then_inc(sem["own_rinv"], 1)
                pool.wait_ge(*at(pool, "own_rinv", u, 1))
                for c0, c1, r in SPANS:
                    last = pool.tensor_tensor(nat[0:r, c0:c1, :], nat[0:r, c0:c1, :],
                                              rinv[0:r, c0:c1].unsqueeze(2).broadcast_to([r, c1 - c0, D]), ALU.mult)
                last.then_inc(sem["ctx_normal"], 1)

            def stage(s, n):
                if s.prep is not None:
                    for g in range(3):
                        low_part(s.prep, g, ctf, ct[:, s.prep.par], "ct_read", "ct_lo")
                if s.att2 is not None:
                    spread2(s.att2)
                if s.prep is not None:
                    for g in range(3):
                        low_part(s.prep, g, kf, kp, "k_read", "k_lo")
                if s.post is not None and s.post.L:
                    root(s.post)
                if s.load is not None and s.load.L == 0:
                    squares(s.load)
                if s.prep is not None:
                    spread(s.prep, s.top)
                if s.load is not None and s.load.L == 0:
                    normalise(s.load)
                if s.att2 is not None:
                    less_maximum(s.att2)
                    root(s.att2)

            pool.memset(half[:, :], -0.5).then_inc(sem["pool_ready"], 1)
            pipeline(pool, UNITS, stage, last=-3)
            for i in range(2):
                pool.memset(vx[:, i, :, :], 0.0).then_inc(sem["pool_ready"], 1)
                pool.wait_ge(sem["pool_ready"], 2 + 2 * i)
                pool.memset(vx[:, i, :, 0:2 * (DH + 1)].rearrange("p a (f e) -> p a f e", f=2)[:, :, :, DH:DH + 1], 1.0
                            ).then_inc(sem["pool_ready"], 1)
                pool.wait_ge(sem["pool_ready"], 3 + 2 * i)
            pool.memset(v2[:, :, DH:DH + 1], 1.0).then_inc(sem["pool_ready"], 1)
            pool.wait_ge(sem["x_power"], 1)
            pool.tensor_tensor(rinvx[:, :], ssqx[:, :], half[0:S, 0:B], ALU.pow).then_inc(sem["x_root"], 1)
            pipeline(pool, UNITS, stage, first=-2)

        @block.tensor
        def _(pe):
            def begin(use, u):
                await_read(pe, bank(use, u))
                held[bank(use, u)] = (use, u)
                return shared[bank(use, u)]

            def context(u, g):
                if g == 0:
                    pe.wait_ge(*at(pe, "ctx_normal", u, 1) if u.L == 0 else
                               at(pe, "ctx_loaded", u, PER["ctx_loaded"][u.L]))
                ps = begin(f"ct{g}", u)
                chunks, c0, _, r = groups()[g]
                for c in chunks:
                    to = chunk(c)[0] - c0
                    last = pe.transpose(ps[:, to:to + r], nat[0:r, c, :], ident[0:r, 0:r])
                last.then_inc(sem["ct_filled"], 1)

            def keys(u, g):
                if u is UNITS[0] and g == 0:
                    pe.wait_ge(sem["wk_ready"], 1)
                pe.wait_ge(*at(pe, "ct_lo", u, g + 1))
                ps = begin(f"k{g}", u)
                _, c0, n, _ = groups()[g]
                for j, (w, c) in enumerate(((0, 0), (0, 1), (1, 0))):
                    last = pe.matmul(ps[:, 0:n], wk16[:, w, u.L, :], ct[:, u.par, c, c0:c0 + n], start=(j == 0),
                                     stop=(j == 2))
                last.then_inc(sem["k_filled"], 1)

            def vals(u, g):
                if u is UNITS[0] and g == 0:
                    pe.wait_ge(sem["rest_ready"], 1)
                ps = begin(f"v{g}", u)
                for i, c in enumerate(groups()[g][0]):
                    c0, r = chunk(c)
                    for j, (w, p) in enumerate(((0, 0), (1, 0), (0, 1))):
                        last = pe.matmul(ps[0:r, D * i:D * i + D], ct[:, u.par, p, c0:c0 + r], wv16[:, w, u.L, :],
                                         start=(j == 0), stop=(j == 2))
                last.then_inc(sem["v_filled"], 1)

            def mask(u, g):
                if g == 0:
                    pe.wait_ge(*at(pe, "mask_copied", u, 1))
                ps = begin(f"mk{g}", u)
                for i, c in enumerate(GROUPS[g]):
                    last = pe.transpose(ps[0:ROWS[c], :].bitcast(BF16)[:, S * i:S * i + S],
                                        maskb[:, c:c + NCH * (ROWS[c] - 1) + 1:NCH], identb[0:S, 0:S])
                last.then_inc(sem["mk_filled"], 1)

            def inputs(u):
                pe.wait_ge(*at(pe, "x_copied", u, 1))
                ps = begin("xT", u)
                pe.transpose(ps[:, 0:S], xcur[:, :], ident[0:S, 0:S]).then_inc(sem["xT_filled"], 1)

            def queries(u):
                pe.wait_ge(*at(pe, "x_lo", u, 1))
                ps = begin("q", u)
                for t in range(T):
                    for j, (w, p) in enumerate(((0, 0), (0, 1), (1, 0))):
                        last = pe.matmul(ps[0:PARTS, S * t:S * t + S], wq16[:, w, u.L, t, :], xT[:, p, :],
                                         start=(j == 0), stop=(j == 2))
                last.then_inc(sem["q_filled"], 1)

            def add_mask(ps, tile, which, c, r):
                return pe.matmul(ps.rearrange("p (h s) -> p h s", h=HT), masked_by[0:r, which, 0:r],
                                 tile[0:r, c, :].unsqueeze(1).broadcast_to([r, HT, S]), start=False, stop=True)

            def max_scores(u, j, masks):
                c, t = divmod(j, T)
                c0, r = chunk(c)
                if j == 0:
                    pe.wait_ge(*at(pe, "q_spread", u, 1))
                    pe.wait_ge(*at(pe, "m_ready", u, 0))
                    if masks:
                        pe.wait_ge(*at(pe, "mask_ready", u, 3))
                if c % 4 == 0 and t == 0:
                    pe.wait_ge(*at(pe, f"krep_in{c // 4}", u, 16 * 12))
                pe.wait_ge(*at(pe, "smax_used", u, j - MR + 1))
                ps = smax[j % MR][0:r, 0:QW]
                last = pe.matmul(ps, krep[0:PARTS, u.par, t, c0:c0 + r],
                                 qmax[:, u.par, t, :, :].rearrange("p h s -> p (h s)"), start=True, stop=not masks)
                if masks:
                    last = add_mask(ps, maskmax[:, u.par], 0, c, r)
                last.then_inc(sem["smax_ready"], 1)

            def maxima(u):
                n = chunk(0)[1]
                pe.wait_ge(*at(pe, "smax_used", u, NSTEP))
                for i in range(2):
                    for h in range(8):
                        last = pe.transpose(smax[i][0:S, :].bitcast(F16)[:, 128 * h:128 * h + n],
                                            mx[0:n, S * (8 * i + h):S * (8 * i + h) + S], ident16[0:n, 0:n])
                    last.then_inc(sem["mt_filled"], 1)

            def maximum_rows(u):
                pe.wait_ge(*at(pe, "m_ready", u, 2))
                ps = begin("mn", u)
                pe.transpose(ps[0:H, :].bitcast(F16)[:, 0:S], mneg[:, :], ident16[0:S, 0:S]
                             ).then_inc(sem["mn_filled"], 1)

            def exp_scores(u, j, masks):
                c, t = divmod(j, T)
                c0, r = chunk(c)
                if u is UNITS[0] and j == 0:
                    pe.wait_ge(sem["ones_ready"], 1)
                if j == 0:
                    pe.wait_ge(*at(pe, "mrow_in", u, 16))
                    pe.wait_ge(*at(pe, "qexp_in", u, 16))
                    if u.L == 1:
                        pe.wait_ge(*at(pe, "maskexp_in", u, 32))
                pe.wait_ge(*at(pe, "probs_ready", u, j - SR + 1))
                ps = sexp[j % SR][0:r, 0:QW]
                last = pe.matmul(ps, krep[:, u.par, t, c0:c0 + r],
                                 qexp[:, u.par, t, :, :].rearrange("p h s -> p (h s)"), start=True, stop=not masks)
                if masks:
                    last = add_mask(ps, maskexp[:, u.par], 1, c, r)
                last.then_inc(sem["sexp_ready"], 1)

            def values(u, j):
                c, t = divmod(j, T)
                r = chunk(c)[1]
                if j == 0:
                    pe.wait_ge(*at(pe, "v_ready", u, NG[u.L]))
                    pe.wait_ge(*at(pe, "acc_copied", u, 0))
                if j >= NSTEP - PVLAG:
                    pe.wait_ge(*at(pe, "probs_ready", u, j + 1))
                for p in range(2):
                    q, slot = 2 * (t % 2) + p, t // 2
                    last = pe.matmul(acc[32 * q:32 * q + VW, 2 * S * slot:2 * S * slot + 2 * S],
                                     vx[0:r, u.par, PAIRS * c + 2 * t + p, :],
                                     probs[0:r, j % PR, 2 * S * p:2 * S * p + 2 * S],
                                     start=(c == 0 and slot == 0), stop=(c == NCH - 1), skip_group_check=True)
                last.then_inc(sem["pv_done"], 1)

            def output(u):
                pe.wait_ge(*at(pe, "acc_copied", u, 1))
                ps = begin("O", u)
                for t in range(T):
                    last = pe.transpose(ps[0:S, 128 * t:128 * t + 128], osb[:, S * t:S * t + S], ident[:, :])
                last.then_inc(sem["o_filled"], 1)

            def output_back(u):
                pe.wait_ge(*at(pe, "o_normal" if u.L else "o_read", u, 1))
                ps = begin("OT", u)
                pe.transpose(ps[:, 0:S], oatt[:, 0, :], ident[0:S, 0:S]).then_inc(sem["oT_filled"], 1)

            def project(u):
                pe.wait_ge(*at(pe, "oT_ready", u, 1))
                ps = begin("wo", u)
                pe.matmul(ps[0:S, 0:D], oT[:, :], wo[:, u.L, :], start=True, stop=True).then_inc(sem["wo_filled"], 1)

            def context_input2(u):
                pe.wait_ge(*at(pe, "nat2_in", u, 32))
                ps = begin("cx2", u)
                pe.transpose(ps[:, 0:S], nat2[:, :], ident[0:S, 0:S])
                pe.transpose(ps[:, S:2 * S], x2[:, :], ident[0:S, 0:S]).then_inc(sem["cx2_filled"], 1)

            def keys_queries_values2(u):
                pe.wait_ge(*at(pe, "cx2_read", u, 1))
                ps = begin("kqv2", u)
                pe.matmul(ps[:, 0:S], wk[:, 2, :], cx2[:, 0, :], start=True, stop=True)
                for t in range(T):
                    pe.matmul(ps[32 * t:32 * t + 32, S:2 * S], wq[:, 2, t, 0:32], cx2[:, 1, :], start=True, stop=True)
                pe.matmul(ps[0:S, 2 * S:2 * S + D], cx2[:, 0, :], wv[:, 2, :], start=True, stop=True
                          ).then_inc(sem["kqv2_filled"], 1)

            def scores2(u, t):
                if t == 0:
                    pe.wait_ge(*at(pe, "kbd2_ready", u, 1))
                ps = begin(f"s2{t}", u)
                pe.matmul(ps[0:S, 0:QW], q2[:, :], kbd2[:, HT * t:HT * t + HT, :].rearrange("p h s -> p (h s)"),
                          start=True, stop=True).then_inc(sem["s2_filled"], 1)

            def transposed2(u, t):
                if t == 0:
                    pe.wait_ge(*at(pe, "exp2_ready", u, 1))
                ps = begin(f"pt2{t}", u)
                for h in range(HT):
                    last = pe.transpose(ps[0:S, S * h:S * h + S], sc2[:, HT * t + h, :], ident[0:S, 0:S])
                last.then_inc(sem["pt2_filled"], 1)

            def values2(u, t):
                if t == 0:
                    pe.wait_ge(*at(pe, "pt2_read", u, T))
                    begin("o2", u)
                ps = shared[bank("o2", u)]
                for h in range(HT * t, HT * t + HT):
                    last = pe.matmul(ps[0:S, (DH + 1) * h:(DH + 1) * h + DH + 1], pT2[:, h, :], v2[:, h, :], start=True,
                                     stop=True)
                if t == T - 1:
                    last.then_inc(sem["o2_filled"], 1)

            def attention_back2(u):
                pe.wait_ge(*at(pe, "att2_ready", u, 1))
                ps = begin("at2", u)
                pe.transpose(ps[:, 0:S], att2[:, :], ident[0:S, 0:S]).then_inc(sem["at2_filled"], 1)

            def hidden2(u):
                pe.wait_ge(*at(pe, "at2_read", u, 1))
                ps = begin("h2", u)
                for j in range(FF // 128):
                    last = pe.matmul(ps[:, S * j:S * j + S], w1[:, 128 * j:128 * j + 128], aT2[:, :], start=True, stop=True)
                last.then_inc(sem["h2_filled"], 1)

            def feed_forward2(u):
                pe.wait_ge(*at(pe, "h2_read", u, FF // 128))
                ps = begin("w2", u)
                for j in range(FF // 128):
                    last = pe.matmul(ps[0:S, 0:D], hT[:, j, :], w2[:, j, :], start=(j == 0), stop=(j == FF // 128 - 1))
                last.then_inc(sem["w2_filled"], 1)

            def layer2(s, j):
                if s.att2 is not None:
                    if j == AT2["cx"]:
                        context_input2(s.att2)
                    if j == AT2["kqv"]:
                        keys_queries_values2(s.att2)
                    for t in range(T):
                        if j == AT2[f"s{t}"]:
                            scores2(s.att2, t)
                        if j == AT2[f"pt{t}"]:
                            transposed2(s.att2, t)
                    for t in range(T):
                        if j == AT2["o"] - T + 1 + t:
                            values2(s.att2, t)
                if s.ff2 is not None:
                    if j == AT2_FF["at"]:
                        attention_back2(s.ff2)
                    if j == AT2_FF["h"]:
                        hidden2(s.ff2)
                    if j == AT2_FF["w2"]:
                        feed_forward2(s.ff2)

            def flag_sum():
                pe.wait_ge(sem["mask_counted"], 1)
                ps = begin("flag", None)
                pe.matmul(ps[0:1, 0:1], maskcount[:, :], ones[:, :], start=True, stop=True
                          ).then_inc(sem["flag_filled"], 1)

            def stage(s, n, masks=False):
                for j in range(NSTEP):
                    if s.exp is not None:
                        exp_scores(s.exp, j, masks and s.exp.L == 1)
                    for i in range(NSTEP):
                        if MAX_AT[i] == j and s.top is not None:
                            max_scores(s.top, i, masks and s.top.L == 1)
                    if s.post is not None and j < PVLAG:
                        values(s.post, NSTEP - PVLAG + j)
                    for i in range(NSTEP):
                        if VALUES_AT[i] == j and s.exp is not None:
                            values(s.exp, i)
                    for g in range(3):
                        if s.prep is not None and j == AT[f"ct{g}"]:
                            context(s.prep, g)
                        if s.prep is not None and j == AT[f"k{g}"]:
                            keys(s.prep, g)
                        if s.prep is not None and s.prep.L == 1 and j == AT[f"mk{g}"]:
                            mask(s.prep, g)
                        if s.top is not None and j == AT[f"v{g}"]:
                            vals(s.top, g)
                    if s.post is not None and j == AT["O"]:
                        output(s.post)
                    if s.post is not None and s.post.L < 3 and j == AT["OT"]:
                        output_back(s.post)
                    if s.post is not None and s.post.L < 3 and j == AT["wo"]:
                        project(s.post)
                    if s.prep is not None and j == AT["xT"]:
                        inputs(s.prep)
                    if s.prep is not None and j == AT["q"]:
                        queries(s.prep)
                    if s.top is not None and j == MT_AT:
                        maxima(s.top)
                    if s.top is not None and j == AT["mn"]:
                        maximum_rows(s.top)
                    layer2(s, j)
                    if n == FLAG_STAGE and j == NSTEP - 1:
                        flag_sum()

            pe.wait_ge(sem["const_in"], 16 * 14)
            pipeline(pe, UNITS, stage, last=MASK_STAGES[0] - 1)
            flag = pe.value_load(maskflag[0:1, 0:1])
            before = list(held)
            with pe.If(flag != 0):
                pipeline(pe, UNITS, lambda s, n: stage(s, n, masks=True), *MASK_STAGES)
            held[:] = before
            with pe.Else():
                pipeline(pe, UNITS, stage, *MASK_STAGES)
            pipeline(pe, UNITS, stage, first=MASK_STAGES[1] + 1)
            held[:] = [None, None]

        @block.scalar
        def _(act):
            def context(u, g, part):
                _, c0, n, _ = groups()[g]
                if part == 0:
                    act.wait_ge(*at(act, "ct_filled", u, g + 1))
                    if g == 0:
                        act.wait_ge(*at(act, "ct_lo", u, 0))
                dst, src = (ctf[:, c0:c0 + n], ct[:, u.par, 0, c0:c0 + n])[part], shared[bank(f"ct{g}", u)][:, 0:n]
                op = act.copy(dst, src) if u.L else act.mul(dst, src, cols[:, COLC["gkv"]:COLC["gkv"] + 1])
                if part == 1:
                    op.then_inc(sem["ct_read"], 1)

            def keys(u, g, part):
                _, c0, n, _ = groups()[g]
                if part == 0:
                    if g == 0:
                        for i in range(3):
                            act.wait_ge(*at(act, f"krep_in{i}", u, 0))
                    act.wait_ge(*at(act, "k_filled", u, g + 1))
                dst, src = (kf[:, c0:c0 + n], kp[:, 0, c0:c0 + n])[part], shared[bank(f"k{g}", u)][:, 0:n]
                bk = COLC[f"bk{u.L}"] if u.L else 0
                op = act.activation(dst, src, ACT.Identity, bias=cols[:, bk:bk + 1]) if u.L else act.copy(dst, src)
                if part == 1:
                    op.then_inc(sem["k_read"], 1)

            def vals(u, g):
                chunks, _, _, r = groups()[g]
                if u is UNITS[0]:
                    act.wait_ge(sem["pool_ready"], 6)
                act.wait_ge(*at(act, "v_filled", u, g + 1))
                a0, a1 = PAIRS * chunks[0], PAIRS * (chunks[-1] + 1)
                act.copy(vx[0:r, u.par, a0:a1, 0:2 * (DH + 1)].rearrange("p a (f e) -> p a f e", f=2)[:, :, :, 0:DH],
                         shared[bank(f"v{g}", u)][0:r, 0:2 * DH * (a1 - a0)].rearrange("p (a f d) -> p a f d", f=2, d=DH)
                         ).then_inc(sem["v_ready"], 1)

            def mask_bytes(u):
                act.wait_ge(*at(act, "mask_loaded", u, 16))
                act.copy(maskb[:, :], mask8[:, :]).then_inc(sem["mask_copied"], 1)

            def mask(u, g):
                c0, r = GROUPS[g][0], ROWS[GROUPS[g][0]]
                act.wait_ge(*at(act, "mk_filled", u, g + 1))
                act.copy(maskmax[0:r, u.par, c0:c0 + 4, :], shared[bank(f"mk{g}", u)][0:r, :].bitcast(BF16)[:, 0:4 * S].rearrange(
                    "p (c s) -> p c s", c=4)).then_inc(sem["mask_ready"], 1)

            def input_copy(u):
                if u is UNITS[0]:
                    act.wait_ge(sem["x_ready"], 1)
                if u.L:
                    act.wait_ge(*(at(act, "x_next", Unit(0, u.batch, u.reg, 0), 1) if u.L == 1 else
                                  at(act, "x2_next", Unit(2, u.batch, u.reg, 0), 1)))
                act.copy(xcur[:, :], u.rows_of(xall)
                         ).then_inc(sem["x_copied"], 1)

            def inputs(u):
                act.wait_ge(*at(act, "xT_filled", u, 1))
                act.copy(xT[:, 0, :], shared[bank("xT", u)][:, 0:S]).then_inc(sem["x_hi"], 1)

            def maximum_rows(u):
                act.wait_ge(*at(act, "mn_filled", u, 1))
                act.wait_ge(*at(act, "mrow_in", u, 0))
                act.copy(mrow[:, :], shared[bank("mn", u)][0:H, :].bitcast(F16)[:, 0:S]).then_inc(sem["mrow_ready"], 1)

            def exps(u, j):
                r = chunk(j // T)[1]
                act.wait_ge(*at(act, "pv_done", u, j - PR + 1))
                act.wait_ge(*at(act, "sexp_ready", u, j + 1))
                act.activation(probs[0:r, j % PR, :], sexp[j % SR][0:r, 0:QW], ACT.Exp).then_inc(sem["probs_ready"], 1)

            def accumulated(u):
                act.wait_ge(*at(act, "pv_done", u, STEPS[u.L]))
                act.copy(osb[:, :], acc[:, 0:QW]).then_inc(sem["acc_copied"], 1)

            def output_back(u):
                act.wait_ge(*at(act, "oT_filled", u, 1))
                act.copy(oT[:, :], shared[bank("OT", u)][:, 0:S]).then_inc(sem["oT_ready"], 1)

            def layer2(s, j):
                u = s.att2
                if u is not None:
                    if j == AT2["cx"]:
                        act.wait_ge(*at(act, "cx2_filled", u, 1))
                        act.copy(cx2[:, :, :].rearrange("p a s -> p (a s)"), shared[bank("cx2", u)][:, 0:2 * S]).then_inc(sem["cx2_read"], 1)
                    if j == AT2["kqv"]:
                        act.wait_ge(*at(act, "kqv2_filled", u, 1))
                        act.activation(k2[:, :], shared[bank("kqv2", u)][:, 0:S], ACT.Identity, bias=cols[:, COLC["bk2"]:COLC["bk2"] + 1])
                        act.activation(q2[:, :], shared[bank("kqv2", u)][:, S:2 * S], ACT.Identity, bias=bq2[:, :], scale=SCALE)
                        act.copy(v2[:, :, 0:DH], shared[bank("kqv2", u)][0:S, 2 * S:2 * S + D].rearrange("s (h d) -> s h d", d=DH)
                                 ).then_inc(sem["kqv2_read"], 1)
                    if j == AT2["exp"]:
                        act.wait_ge(*at(act, "less2_ready", u, 1))
                        act.activation(sc2[:, :, :], sc2[:, :, :], ACT.Exp).then_inc(sem["exp2_ready"], 1)
                    for t in range(T):
                        if j == AT2[f"pt{t}"]:
                            act.wait_ge(*at(act, "pt2_filled", u, t + 1))
                            act.copy(pT2[:, HT * t:HT * t + HT, :].rearrange("p h s -> p (h s)"), shared[bank(f"pt2{t}", u)][0:S, 0:QW]
                                     ).then_inc(sem["pt2_read"], 1)
                u = s.ff2
                if u is not None:
                    if j == AT2_FF["at"]:
                        act.wait_ge(*at(act, "at2_filled", u, 1))
                        act.copy(aT2[:, :], shared[bank("at2", u)][:, 0:S]).then_inc(sem["at2_read"], 1)
                    if j == AT2_FF["h"]:
                        act.wait_ge(*at(act, "h2_filled", u, 1))
                        for i in range(FF // 128):
                            k = COLC["ffb0"] + i
                            act.activation(hT[:, i, :], shared[bank("h2", u)][:, S * i:S * i + S], ACT.Gelu, bias=cols[:, k:k + 1]
                                           ).then_inc(sem["h2_read"], 1)

            def stage(s, n):
                for j in range(NSTEP):
                    if s.exp is not None:
                        exps(s.exp, j)
                    if s.post is not None and j == ACC_AT:
                        accumulated(s.post)
                    for g in range(3):
                        for part in range(2):
                            if s.prep is not None and j == AT[f"ct{g}"] + part:
                                context(s.prep, g, part)
                            if s.prep is not None and j == AT[f"k{g}"] + part:
                                keys(s.prep, g, part)
                        if s.prep is not None and s.prep.L == 1 and j == AT[f"mk{g}"]:
                            mask(s.prep, g)
                        if s.top is not None and j == AT[f"v{g}"]:
                            vals(s.top, g)
                    if s.post is not None and s.post.L < 3 and j == AT["OT"]:
                        output_back(s.post)
                    if s.prep is not None and j == AT["xT"] - 3:
                        input_copy(s.prep)
                    if s.prep is not None and j == AT["xT"]:
                        inputs(s.prep)
                    if s.prep is not None and s.prep.L == 1 and j == AT["mk0"] - 3:
                        mask_bytes(s.prep)
                    layer2(s, j)
                    if n == FLAG_STAGE - 1 and j == AT["v2"] + 1:
                        act.wait_ge(sem["mask_in_all"], 16)
                        act.activation(anymask[:, :], anymask[:, :], ACT.Copy, accum_out=maskcount[:, :]
                                       ).then_inc(sem["mask_counted"], 1)
                    if s.top is not None and j == AT["mn"]:
                        maximum_rows(s.top)
                    if n == FLAG_STAGE and j == NSTEP - 1:
                        act.wait_ge(sem["flag_filled"], 1)
                        act.copy(maskflag[:, :], shared[BANK["flag"]][0:1, 0:1]).then_inc(sem["flag_ready"], 1)

            act.wait_ge(sem["const_in"], 16 * 14)
            pipeline(act, UNITS, stage)

        @block.vector
        def _(dve):
            counted = {}

            def own(name, u, op):
                counted[name] = counted.get(name, 0) + 1
                assert counted[name] <= PER[name][u.L]
                op.then_inc(sem[name], 1)
                dve.wait_ge(*at(dve, name, u, counted[name]))

            def power(u, part):
                if part == 0:
                    dve.wait_ge(*at(dve, "squares_ready", u, 1))
                c0, c1, r = SPANS[part]
                op = dve.tensor_reduce(ssq[0:r, c0:c1], sq[0:r, c0:c1, :], AX, ALU.add)
                if part == 1:
                    own("own_power", u, op)
                    for c0, c1, r in SPANS:
                        op = dve.tensor_scalar(ssq[0:r, c0:c1], ssq[0:r, c0:c1], 1.0 / D, EPS[0], ALU.mult, ALU.add)
                    op.then_inc(sem["row_power"], 1)

            def inputs(u):
                dve.wait_ge(*at(dve, "x_hi", u, 1))
                dve.tensor_tensor(xT[:, 1, :], shared[bank("xT", u)][:, 0:S], xT[:, 0, :], ALU.subtract).then_inc(sem["x_lo"], 1)

            def queries(u):
                dve.wait_ge(*at(dve, "q_filled", u, 1))
                dve.scalar_tensor_tensor(out=qf[:, :, :], in0=shared[bank("q", u)][0:PARTS, 0:T * S].rearrange("p (t s) -> p t s", t=T),
                                         scalar=SCALE, in1=bqs[:, u.L, :].unsqueeze(2).broadcast_to([PARTS, T, S]),
                                         op0=ALU.mult, op1=ALU.add).then_inc(sem["q_read"], 1)
                dve.wait_ge(*at(dve, "q_read", u, 1))
                dve.wait_ge(*at(dve, "q_spread", u, 0))
                own("own_q", u, dve.tensor_copy(qs[:, :, :], qf[:, :, :]))
                dve.tensor_tensor(qs[32:64, :, :], qf[32:64, :, :], qs[32:64, :, :], ALU.subtract
                                  ).then_inc(sem["q_parts"], 1)

            def maximum(u, i):
                c, t = divmod(i, T)
                r = chunk(c)[1]
                dve.wait_ge(*at(dve, "smax_ready", u, i + 1))
                src, dst = smax[i % MR][0:r, 0:QW], mx[0:r, QW * t:QW * t + QW]
                if c == 0:
                    op = dve.tensor_copy(dst, src)
                else:
                    op = dve.tensor_tensor(dst, src, dst, ALU.max)
                op.then_inc(sem["smax_used"], 1)

            def maxima(u, i):
                dve.wait_ge(*at(dve, "mt_filled", u, i + 1))
                dve.tensor_reduce(mneg[:, 8 * i:8 * i + 8], smax[i][0:S, :].bitcast(F16).rearrange(
                    "s (h n) -> s h n", h=8)[:, :, 0:chunk(0)[1]], AX, ALU.max, negate=True).then_inc(sem["m_ready"], 1)

            def centre(u, src):
                k, own_name, done = (1, "own_2", "var2_ready") if u.L == 2 else (0, "own_ln", "var_ready")
                own(own_name, u, dve.tensor_reduce(mv[:, k, 0:1], src, AX, ALU.add))
                own(own_name, u, dve.scalar_tensor_tensor(out=xn[:, k, :], in0=mv[:, k, 0:1].broadcast_to([S, D]),
                                                          scalar=-1.0 / D, in1=src, op0=ALU.mult, op1=ALU.add))
                own(own_name, u, dve.tensor_tensor_reduce(squared[:, k, :], xn[:, k, :], xn[:, k, :], 1.0, 0.0, ALU.mult,
                                                          ALU.add, mv[:, k, 1:2]))
                dve.tensor_scalar(vare[:, k:k + 1], mv[:, k, 1:2], 1.0 / D, EPS[u.L], ALU.mult, ALU.add
                                  ).then_inc(sem[done], 1)

            def scale(u, dst, done):
                k, own_name, ready = (1, "own_2", "rstd2_ready") if u.L == 2 else (0, "own_ln", "rstd_ready")
                dve.wait_ge(*at(dve, ready, u, 1))
                own(own_name, u, dve.scalar_tensor_tensor(out=xn[:, k, :], in0=xn[:, k, :], scalar=rstd[:, k:k + 1],
                                                          in1=rows[:, ROW[f"g{u.L}"], :], op0=ALU.mult, op1=ALU.mult))
                dve.tensor_tensor(dst, xn[:, k, :], rows[:, ROW[f"b{u.L}"], :], ALU.add).then_inc(sem[done], 1)

            def residual(u):
                return u.rows_of(xall)

            def output(u):
                dve.wait_ge(*at(dve, "o_filled", u, 1))
                o = shared[bank("O", u)][0:S, :].rearrange("s (a f q v) -> s f a q v", a=2, f=2, q=4)
                sums = osum[:, 0, :].rearrange("s (a q f) -> s f a q", a=2, q=4)
                to = oatt[:, 0, :].rearrange("s (a q f d) -> s f a q d", a=2, q=4, f=2)
                for f in range(2):
                    op = dve.reciprocal(sums[:, f], o[:, f, :, :, (DH + 1) * f + DH])
                own("own_o", u, op)
                for f in range(2):
                    op = dve.tensor_tensor(to[:, f], o[:, f, :, :, (DH + 1) * f:(DH + 1) * f + DH],
                                           sums[:, f].unsqueeze(3).broadcast_to([S, 2, 4, DH]), ALU.mult)
                op.then_inc(sem["o_read"], 1)
                if u.L == 0:
                    return
                dve.wait_ge(*at(dve, "o_read", u, 1))
                bv = rows[:, ROW[f"bv{u.L}"], :]
                if u.L == 1:
                    dve.tensor_tensor(oatt[:, 0, :], oatt[:, 0, :], bv, ALU.add).then_inc(sem["o_normal"], 1)
                    return
                own("own_o", u, dve.tensor_tensor(y[:, 0, :], oatt[:, 0, :], bv, ALU.add))
                own("own_o", u, dve.tensor_tensor(y[:, 0, :], y[:, 0, :], residual(u), ALU.add))
                centre(u, y[:, 0, :])

            def projected(u):
                dve.wait_ge(*at(dve, "wo_filled", u, 1))
                dve.tensor_tensor(y[:, 0, :], shared[bank("wo", u)][0:S, 0:D], rows[:, ROW[f"bo{u.L}"], :], ALU.add
                                  ).then_inc(sem["wo_read"], 1)
                dve.wait_ge(*at(dve, "wo_read", u, 1))
                if u.L == 0:
                    dve.tensor_tensor(residual(u), y[:, 0, :], residual(u), ALU.add).then_inc(sem["x_next"], 1)
                    return
                own("own_y", u, dve.tensor_tensor(y[:, 0, :], y[:, 0, :], residual(u), ALU.add))
                centre(u, y[:, 0, :])

            def causal2(u, t):
                dve.wait_ge(*at(dve, "s2_filled", u, t + 1))
                dve.tensor_tensor(sc2[:, HT * t:HT * t + HT, :], shared[bank(f"s2{t}", u)][0:S, 0:QW].rearrange("p (h s) -> p h s", h=HT),
                                  causal[:, :].unsqueeze(1).broadcast_to([S, HT, S]), ALU.add).then_inc(sem["s2_read"], 1)

            def output2(u):
                dve.wait_ge(*at(dve, "o2_filled", u, 1))
                o = shared[bank("o2", u)][0:S, 0:(DH + 1) * H].rearrange("s (h e) -> s h e", h=H)
                own("own_2", u, dve.reciprocal(osum[:, 1, :].unsqueeze(2), o[:, :, DH:DH + 1]))
                dve.tensor_tensor(oatt[:, 1, :].rearrange("s (h d) -> s h d", h=H), o[:, :, 0:DH],
                                  osum[:, 1, :].unsqueeze(2).broadcast_to([S, H, DH]), ALU.mult).then_inc(sem["o2_read"], 1)
                dve.wait_ge(*at(dve, "o2_read", u, 1))
                own("own_2", u, dve.tensor_tensor(y[:, 1, :], oatt[:, 1, :], rows[:, ROW["bv2"], :], ALU.add))
                own("own_2", u, dve.tensor_tensor(y[:, 1, :], y[:, 1, :], residual(u), ALU.add))
                centre(u, y[:, 1, :])

            def feed_forward2(u):
                dve.wait_ge(*at(dve, "w2_filled", u, 1))
                dve.tensor_tensor(y[:, 1, :], shared[bank("w2", u)][0:S, 0:D], rows[:, ROW["ff2"], :], ALU.add
                                  ).then_inc(sem["w2_read"], 1)
                dve.wait_ge(*at(dve, "w2_read", u, 1))
                dve.tensor_tensor(residual(u), y[:, 1, :], att2[:, :], ALU.add).then_inc(sem["x2_next"], 1)

            def layer2(s, j):
                if s.att2 is not None:
                    for t in range(T):
                        if j == AT2[f"s{t}"]:
                            causal2(s.att2, t)
                    if j == AT2["max"]:
                        dve.wait_ge(*at(dve, "s2_read", s.att2, T))
                        dve.tensor_reduce(max2[:, :], sc2[:, :, :], AX, ALU.max, negate=True).then_inc(sem["max2_ready"], 1)
                    if j == AT2["o"] + 1:
                        output2(s.att2)
                    if j == AT2["scale"]:
                        scale(s.att2, att2[:, :], "att2_ready")
                if s.ff2 is not None and j == AT2_FF["w2"] + 1:
                    feed_forward2(s.ff2)

            def stage(s, n):
                counted.clear()
                for j in range(NSTEP):
                    for i in range(NSTEP):
                        if MAX_AT[i] == j and s.top is not None:
                            maximum(s.top, i)
                    if s.post is not None and j == AT["O"] + 1:
                        output(s.post)
                    if s.post is not None and s.post.L < 3 and j == AT["wo"] + 1:
                        projected(s.post)
                    if s.prep is not None and j == AT["xT"]:
                        inputs(s.prep)
                    if s.prep is not None and j == AT["q"]:
                        queries(s.prep)
                    if s.post is not None and s.post.L == 1 and j == AT["q"] + 3:
                        scale(s.post, residual(s.post), "x_next")
                    if s.post is not None and s.post.L == 3 and j == AT["q"] + 3:
                        dve.wait_ge(*at(dve, "out_sent", s.post, 0))
                        scale(s.post, outsb[:, :], "out_ready")
                    for part in range(2):
                        if s.load is not None and s.load.L == 0 and j == AT["v2"] + 3 + 3 * part:
                            power(s.load, part)
                    if s.top is not None and j == MT_AT:
                        for i in range(2):
                            maxima(s.top, i)
                    layer2(s, j)

            steps = [0]

            def step(op):
                steps[0] += 1
                op.then_inc(sem["setup"], 1)
                dve.wait_ge(sem["setup"], steps[0])

            dve.memset(krep[PARTS:PARTS + 1, :, :, :].rearrange("o a t k -> o (a t k)").bitcast(F32), TWO_ONES
                       ).then_inc(sem["ones_ready"], 1)
            pipeline(dve, UNITS, stage, last=-3)
            dve.wait_ge(sem["const_in"], 16 * 14)

            def split(w, high, low):
                step(dve.tensor_copy(high, w))
                return dve.tensor_tensor(low, w, high, ALU.subtract)

            split(wk[:, :, :], wk16[:, 0], wk16[:, 1]).then_inc(sem["wk_ready"], 1)
            sqx = kbd2[0:S, :, :].rearrange("s h k -> s (h k)")[:, 0:B * D].rearrange("s (b d) -> s b d", d=D)
            step(dve.tensor_tensor(sqx, xall[:, :, :], xall[:, :, :], ALU.mult))
            step(dve.tensor_reduce(ssqx[:, :], sqx, AX, ALU.add))
            dve.tensor_scalar(ssqx[:, :], ssqx[:, :], 1.0 / D, EPS[0], ALU.mult, ALU.add).then_inc(sem["x_power"], 1)
            split(wq[:, :, :, :], wq16[:, 0], wq16[:, 1])
            dve.tensor_copy(headmask16[:, :], headmask[:, :])
            dve.tensor_scalar(bqs[:, :, :], bq[:, :, :], SCALE, None, ALU.mult)
            dve.wait_ge(sem["x_root"], 1)
            step(dve.tensor_tensor(xall[:, :, :], xall[:, :, :], rinvx[:, :].unsqueeze(2).broadcast_to([S, B, D]), ALU.mult))
            dve.tensor_tensor(xall[:, :, :], xall[:, :, :],
                              rows[:, ROW["gq"], :].unsqueeze(1).broadcast_to([S, B, D]), ALU.mult
                              ).then_inc(sem["x_ready"], 1)
            split(wv[:, :, :], wv16[:, 0], wv16[:, 1])
            dve.tensor_copy(ident16[:, :], ident[:, :])
            dve.tensor_copy(identb[:, :], ident[:, :])
            for i in range(2):
                dve.tensor_scalar(masked_by[:, i, :], ident[:, :], MASKED[i], None, ALU.mult)
            dve.tensor_scalar(bq2[:, :], cols[:, COLC["bq2"]:COLC["bq2"] + 1], SCALE, None, ALU.mult)
            dve.memset(ones[:, :], 1.0).then_inc(sem["rest_ready"], 1)
            pipeline(dve, UNITS, stage, first=-2)


def kernel(**inputs):
    import concourse.bacc as _bacc
    from concourse.bass_utils import run_bass_kernel_spmd as _run

    a = {k: np.asarray(v) for k, v in inputs.items()}
    wq = np.stack([a["L0_xattn_wq"].T, a["L1_xattn_Wq"].T, a["L2_xattn_Wq"].T, a["L3_xattn_Wq"]])
    wk = np.stack([a["L0_xattn_wk"].T, a["L1_xattn_Wk"].T, a["L2_xattn_Wk"].T, a["L3_xattn_Wk"]])
    wv = np.stack([a["L0_xattn_wv"].T, a["L1_xattn_Wv"].T, a["L2_xattn_Wv"].T, a["L3_xattn_Wv"]])
    wq3 = np.concatenate([wq.reshape(4, D, T, 1, 32)] * 3, axis=3).reshape(4, D, T * PARTS)
    row = {"gq": "L0_xattn_gq", "bo0": "L0_xattn_bo", "bv1": "L1_xattn_bv", "bo1": "L1_xattn_bo",
           "g1": "L1_xattn_gamma", "b1": "L1_xattn_beta", "bv2": "L2_xattn_bv", "g2": "L2_xattn_ln_g",
           "b2": "L2_xattn_ln_b", "ff2": "L2_xattn_b2", "bv3": "L3_xattn_bv", "g3": "L3_xattn_ln_gamma",
           "b3": "L3_xattn_ln_beta"}
    rows = np.stack([a[row[n]] for n in ROW])
    b1 = a["L2_xattn_b1"].reshape(FF // 128, 128)
    cols = np.stack([a["L0_xattn_gkv"], a["L1_xattn_bk"], a["L2_xattn_bk"], a["L3_xattn_bk"], a["L2_xattn_bq"],
                     *b1], axis=1)
    zero = np.zeros(D, np.float32)
    bq = np.stack([zero, a["L1_xattn_bq"], a["L2_xattn_bq"], a["L3_xattn_bq"]]).reshape(4, T, 1, 32)
    bq = np.concatenate([bq] * 3, axis=2).reshape(4, T, PARTS).transpose(2, 0, 1)
    headmask = np.zeros((PARTS, HT), np.float32)
    for p in range(PARTS):
        headmask[p, p % 32 // DH] = 1.0
    heads = np.repeat(np.eye(H, dtype=np.float32), DH, axis=0)
    causal = np.where(np.arange(S)[None, :] > np.arange(S)[:, None], -1e9, 0).astype(np.float32)
    arrays = {
        "ctx": a["ctx_1024"], "x": a["x"], "mask": a["mask_Bx1xSxS2_bf0"], "w_qkv": np.concatenate([wq3, wk, wv], axis=2),
        "w_o": np.stack([a["L0_xattn_wo"].T, a["L1_xattn_Wo"].T]), "w_1": a["L2_xattn_W1"].T, "w_2": a["L2_xattn_W2"].T,
        "rows": np.broadcast_to(rows, (S,) + rows.shape), "cols": cols, "bq": bq, "headmask": headmask, "heads": heads,
        "ident": np.eye(128, dtype=np.float32)[None], "causal": causal,
    }
    nc = _bacc.Bacc("TRN2", target_bir_lowering=False, num_devices=1)
    args = []
    for name, value in arrays.items():
        arrays[name] = np.ascontiguousarray(value)
        args.append(nc.dram_tensor(f"in_{name}", value.shape, U8 if name == "mask" else F32, kind="ExternalInput").ap())
    out = nc.dram_tensor("out_0", (B, S, D), F32, kind="ExternalOutput").ap()
    build(nc, *args, out)
    r = _run(nc, [{f"in_{k}": v for k, v in arrays.items()}], core_ids=[0])
    return r.results[0]["out_0"]
```
